# Optimizing a Trainium2 kernel written in Bass

```python
import numpy as np
import jax
import jax.numpy as jnp

def _softmax(x, axis=-1):
    return jax.nn.softmax(x, axis=axis)

def _gelu(x):
    return jax.nn.gelu(x, approximate=True)

def _silu(x):
    return jax.nn.silu(x)

def _sigmoid(x):
    return jax.nn.sigmoid(x)

def _layernorm(x, axis=-1, eps=1e-05):
    m = jnp.mean(x, axis=axis, keepdims=True)
    v = jnp.var(x, axis=axis, keepdims=True)
    return (x - m) / jnp.sqrt(v + eps)

def _scatter_add(tgt, idx, src, axis=0):
    return tgt.at[idx].add(src)

def _segment_sum(src, seg, n):
    return jax.ops.segment_sum(src, seg, n)
kernel_name = 'mk_gnn_ffn_d1_gnn_r8_3f4dca'

def setup_inputs(seed: int=0):
    np.random.seed(seed)
    _w = jnp.asarray

    def _rec_inputs():
        import jax
        import jax.numpy as jnp
        _gk = jax.random.key(seed)
        x = -0.0003713 + 1 * jax.random.normal(jax.random.fold_in(_gk, 1), (6250, 256), jnp.float32)
        src = jax.random.randint(jax.random.fold_in(_gk, 2), (100000,), 0, 6250, jnp.int32)
        dst = jnp.minimum((6250 * jax.random.uniform(jax.random.fold_in(_gk, 3), (100000,)) ** 2.0).astype(jnp.int32), 49999)
        _o = jnp.argsort(dst, stable=True)
        src = src[_o]
        dst = dst[_o]
        return (x, src, dst)
    x, src, dst = _rec_inputs()

    def _L0_gnn_setup():
        import jax, jax.numpy as jnp
        import numpy as np
        N = 6250
        E = 125000
        IN = 256
        H = 4
        D = 64
        OUT = 256
        key = jax.random.key(seed)
        k0, k1, k2, k3, k4 = jax.random.split(key, 5)
        x = jax.random.normal(k0, (N, IN), dtype=jnp.float32)
        edge_index = jax.random.randint(k1, (2, E), 0, N, dtype=jnp.int32)
        W = jax.random.normal(k2, (H, IN, D), dtype=jnp.float32) * 0.05
        attn = jax.random.normal(k3, (H, 2 * D), dtype=jnp.float32) * 0.05
        W_out = jax.random.normal(k4, (H * D, OUT), dtype=jnp.float32) * 0.05
        return {'x': x, 'edge_index': edge_index, 'W': W, 'attn': attn, 'W_out': W_out}
    _L0_gnn_all = _L0_gnn_setup()
    _L0_gnn_in = {k: v for k, v in _L0_gnn_all.items() if k in ('W', 'attn', 'W_out')}
    del _L0_gnn_all

    def _L0_ffn_setup():
        import jax, jax.numpy as jnp
        import numpy as np
        NUM_EXPERTS = 8
        TOP_K = 2
        B, S, D = (8, 1024, 256)

        def _moe(tokens, router_w, w1, b1, w2, b2):
            N = tokens.shape[0]
            E = router_w.shape[0]
            logits = tokens.astype(jnp.float32) @ router_w.astype(jnp.float32).T
            probs = jax.nn.softmax(logits, axis=-1)
            rw, re = jax.lax.top_k(probs, TOP_K)
            if TOP_K > 1:
                rw = rw / jnp.maximum(rw.sum(-1, keepdims=True), 1e-12)
            rw = rw.astype(tokens.dtype)
            combine = jnp.zeros((N, E), tokens.dtype).at[jnp.arange(N)[:, None], re].set(rw)
            out = tokens
            for e in range(E):
                h = jax.nn.gelu(tokens @ w1[e] + b1[e], approximate=False)
                y = h @ w2[e] + b2[e]
                out = out + combine[:, e:e + 1] * y
            return out
        key = jax.random.key(seed)
        ks = jax.random.split(key, 4)
        scale = 1.0 / np.sqrt(D).astype(np.float32)
        return {'input_embeddings': jax.random.normal(ks[0], (B, S, D), jnp.float32), 'router_w': jax.random.normal(ks[1], (NUM_EXPERTS, D), jnp.float32) * scale, 'w1': jax.random.normal(ks[2], (NUM_EXPERTS, D, D), jnp.float32) * scale, 'b1': jnp.zeros((NUM_EXPERTS, D), jnp.float32), 'w2': jax.random.normal(ks[3], (NUM_EXPERTS, D, D), jnp.float32) * scale, 'b2': jnp.zeros((NUM_EXPERTS, D), jnp.float32)}
    _L0_ffn_all = _L0_ffn_setup()
    _L0_ffn_in = {k: v for k, v in _L0_ffn_all.items() if k in ('router_w', 'w1', 'b1', 'w2', 'b2')}
    del _L0_ffn_all
    return {'x': x, 'src': src, 'dst': dst, 'L0_gnn_W': _L0_gnn_in['W'], 'L0_gnn_attn': _L0_gnn_in['attn'], 'L0_gnn_W_out': _L0_gnn_in['W_out'], 'L0_ffn_router_w': _L0_ffn_in['router_w'], 'L0_ffn_w1': _L0_ffn_in['w1'], 'L0_ffn_b1': _L0_ffn_in['b1'], 'L0_ffn_w2': _L0_ffn_in['w2'], 'L0_ffn_b2': _L0_ffn_in['b2']}

def reference(x, src, dst, L0_gnn_W, L0_gnn_attn, L0_gnn_W_out, L0_ffn_router_w, L0_ffn_w1, L0_ffn_b1, L0_ffn_w2, L0_ffn_b2):
    import jax
    import jax.numpy as jnp

    def _L0_gnn_ref(x, edge_index, W, attn, W_out):
        import jax, jax.numpy as jnp
        import numpy as np
        N = 6250
        E = 125000
        IN = 256
        H = 4
        D = 64
        OUT = 256
        src, dst = (edge_index[0], edge_index[1])
        h = jnp.einsum('ni,hid->nhd', x, W)
        h_src = h[src]
        h_dst = h[dst]
        a_src, a_dst = (attn[:, :D], attn[:, D:])
        e = jnp.einsum('ehd,hd->eh', h_src, a_src) + jnp.einsum('ehd,hd->eh', h_dst, a_dst)
        e = jnp.where(e > 0, e, 0.2 * e)
        e_max = jax.ops.segment_max(e, dst, num_segments=N)
        e_stable = jnp.minimum(e - e_max[dst], 20.0)
        alpha = jnp.exp(e_stable)
        alpha_sum = jax.ops.segment_sum(alpha, dst, num_segments=N)
        alpha_norm = alpha / (alpha_sum[dst] + 1e-08)
        msg = alpha_norm[:, :, None] * h_src
        out_h = jax.ops.segment_sum(msg, dst, num_segments=N)
        return out_h.reshape(N, H * D) @ W_out

    def _L0_ffn_ref(input_embeddings, router_w, w1, b1, w2, b2):
        import jax, jax.numpy as jnp
        import numpy as np
        NUM_EXPERTS = 8
        TOP_K = 2
        B, S, D = (8, 1024, 256)

        def _moe(tokens, router_w, w1, b1, w2, b2):
            N = tokens.shape[0]
            E = router_w.shape[0]
            logits = tokens.astype(jnp.float32) @ router_w.astype(jnp.float32).T
            probs = jax.nn.softmax(logits, axis=-1)
            rw, re = jax.lax.top_k(probs, TOP_K)
            if TOP_K > 1:
                rw = rw / jnp.maximum(rw.sum(-1, keepdims=True), 1e-12)
            rw = rw.astype(tokens.dtype)
            combine = jnp.zeros((N, E), tokens.dtype).at[jnp.arange(N)[:, None], re].set(rw)
            out = tokens
            for e in range(E):
                h = jax.nn.gelu(tokens @ w1[e] + b1[e], approximate=False)
                y = h @ w2[e] + b2[e]
                out = out + combine[:, e:e + 1] * y
            return out
        b, s, d = input_embeddings.shape
        tokens = input_embeddings.reshape(b * s, d)
        return _moe(tokens, router_w, w1, b1, w2, b2).reshape(b, s, d)
    edge_index = jnp.stack([src, dst])
    x = x + _L0_gnn_ref(_layernorm(x, axis=-1), edge_index, L0_gnn_W, L0_gnn_attn, L0_gnn_W_out)
    x = x + _L0_ffn_ref(_layernorm(x, axis=-1)[None], L0_ffn_router_w, L0_ffn_w1, L0_ffn_b1, L0_ffn_w2, L0_ffn_b2)[0]
    return x

_drawn_inputs = setup_inputs


def setup_inputs(seed=0):
    import zlib

    import numpy as np

    out = dict(_drawn_inputs(seed))
    spreads = {'L0_ffn_b1': (0.0, 0.328), 'L0_ffn_b2': (0.0, 0.1)}
    factors = {}
    for name, (base, spread) in spreads.items():
        noise = np.random.default_rng([zlib.crc32(name.encode()), seed]).standard_normal(out[name].shape)
        drawn = base * np.exp(spread * noise) if base else spread * noise
        out[name] = jnp.asarray(drawn.astype(out[name].dtype))
    for name, factor in factors.items():
        out[name] = (out[name] * factor).astype(out[name].dtype)
    return out
```

```python
from contextlib import ExitStack

import concourse.bass as bass
from concourse import mybir

F32 = mybir.dt.float32
I32 = mybir.dt.int32
U32 = mybir.dt.uint32
ALU = mybir.AluOpType
ACT = mybir.ActivationFunctionType
AX = mybir.AxisListType.X

P = 128
BIG = 1.0e30
EPS = 1e-5


class Cfg:

    def __init__(self, x, src, W, rw):
        self.N, self.D = x.shape
        self.E = src.shape[0]
        self.H, _, self.DH = W.shape
        self.NE = rw.shape[0]
        self.NB = -(-self.N // P)
        self.TAIL = self.N - (self.NB - 1) * P
        self.BT = 16
        self.NT = -(-self.E // (P * self.BT)) * self.BT
        self.NBAT = self.NT // self.BT
        self.KC = self.D // P
        self.HW = self.DH + 1
        self.ROW = self.H * self.HW
        self.G = -(-self.NT // P)


def gnn_ffn_kernel(nc, x, src, dst, W, attn, W_out, rw, w1, b1, w2, b2, out):
    c = Cfg(x, src, W, rw)
    N, D, E, H, DH, NE, NB, NT, BT, NBAT = c.N, c.D, c.E, c.H, c.DH, c.NE, c.NB, c.NT, c.BT, c.NBAT
    KC, HW, ROW, G, TAIL = c.KC, c.HW, c.ROW, c.G, c.TAIL
    RING = 3
    WIDE = ROW + H
    ZW = BT * H
    full_tiles = E // P
    rest = E - full_tiles * P
    gl = G - 1
    last_full = full_tiles - gl * P
    GB = 7
    GROUPS = NB // GB
    assert GROUPS * GB == NB and G <= P
    L2BASE = NT * P
    L3BASE = L2BASE + G * P
    NONE = L3BASE + P
    LOOK = 2 * P + 4

    def internal(name, shape):
        return nc.dram_tensor(name, shape, F32, kind="Internal").ap()

    table = internal("table", (NB * P, WIDE))
    flag1_d = internal("flag1_d", (NT, 2 * P))
    flag2_d = internal("flag2_d", (G, 2 * P))
    flag3_d = internal("flag3_d", (1, 2 * P))
    last_d = internal("last_d", (G * P,))
    look_d = internal("look_d", (G * P, LOOK))
    start_d = internal("start_d", (G * P * P, H))
    part_d = internal("part_d", (NONE + 1, WIDE))

    with ExitStack() as ctx:
        def sb(name, shape, dt=F32):
            return ctx.enter_context(nc.sbuf_tensor(name, shape, dt))

        def sem(name):
            return ctx.enter_context(nc.semaphore(name))

        bank = [ctx.enter_context(nc.psum_tensor(f"bank{i}", [P, 512], F32)) for i in range(8)]

        ident = sb("ident", [P, P])
        wout_sb = sb("wout_sb", [P, KC, D])
        w1_sb = sb("w1_sb", [P, NE, KC, D])
        w2_sb = sb("w2_sb", [P, NE, KC, D])
        b1_sb = sb("b1_sb", [P, NE, KC])
        b2_sb = sb("b2_sb", [NE, D])
        rwr = sb("rwr", [NE, D])
        rwT = sb("rwT", [P, KC, NE])
        eps_sb = sb("eps_sb", [P, 1])
        ones = sb("ones", [1, P])
        srcC = sb("srcC", [P, G * P], I32)
        rankC = sb("rankC", [P, G * P])
        startC = sb("startC", [P, G * P])
        rank2C = sb("rank2C", [P, G])
        start2C = sb("start2C", [P, G])
        rank3C = sb("rank3C", [P, 1])
        start3C = sb("start3C", [P, 1])
        De = sb("De", [P, NT, H])
        rowsN = sb("rowsN", [P, 3, NB], I32)

        pre = ExitStack()
        ctx.enter_context(pre)

        def s1(name, shape, dt=F32):
            return pre.enter_context(nc.sbuf_tensor(name, shape, dt))

        dN = s1("dN", [P, NB, H])
        cI = s1("cI", [P, NB], I32)
        cF = s1("cF", [P, NB])
        nodecol = s1("nodecol", [P, NB])
        firstI = s1("firstI", [P, G], I32)
        start = s1("start", [P, G, P])
        nofirst = s1("nofirst", [P, G, P])
        with ExitStack() as st:
            def s1(name, shape, dt=F32):
                return st.enter_context(nc.sbuf_tensor(name, shape, dt))

            def sem1(name):
                return st.enter_context(nc.semaphore(name))

            xall = s1("xall", [P, NB, D])
            dstI = s1("dstI", [P, G, P], I32)
            srcI = s1("srcI", [P, G, P], I32)
            dstF = s1("dstF", [P, G, P])
            srcF = s1("srcF", [P, G, P])
            rank = s1("rank", [P, G, P])
            prevI = s1("prevI", [P, G], I32)
            prevF = s1("prevF", [P, G])
            cont = s1("cont", [P, G])
            kF = s1("kF", [P, G, 2, P])
            key2 = s1("key2", [P, G])
            tcol = s1("tcol", [P, G])
            base2 = s1("base2", [P, G])
            k2r = s1("k2r", [G, 1, P])
            start2 = s1("start2", [G, 1, P])
            rank2 = s1("rank2", [G, 1, P])
            kF2 = s1("kF2", [G, 1, 2, P])
            k3r = s1("k3r", [1, 1, P])
            gi = s1("gi", [1, P])
            eq3 = s1("eq3", [1, G])
            last2 = s1("last2", [1, G])
            start3 = s1("start3", [1, 1, P])
            rank3 = s1("rank3", [1, 1, P])
            kF3 = s1("kF3", [1, 1, 2, P])
            rec3 = s1("rec3", [1, 2, G])
            rec = s1("rec", [P, G, 4])
            lastrow = s1("lastrow", [P, NT])
            junk = s1("junk", [P, 2, NT])
            none_row = s1("none_row", [1, WIDE])
            wcat = s1("wcat", [P, KC, WIDE])
            wraw = s1("wraw", [P, KC, H, DH])
            attb = s1("attb", [P, H, 2 * DH])
            wprod = s1("wprod", [P, KC, H, DH])
            stat = s1("stat", [P, NB, 6])
            mv = s1("mv", [P, NB, 2])
            sd = s1("sd", [P, NB])
            rstd = s1("rstd", [P, NB])
            xn1 = s1("xn1", [P, 2, D])
            xnT = s1("xnT", [P, 2, KC, P])
            hrow = s1("hrow", [P, 2, WIDE])
            (pads, ld_x, ld_e, ld_w, ld_ffn, ident_ok, iota_ok, dv, count_ok, idx_t, key2_ok, key2_t, rank2_ok, rank2_t,
             rank3_ok, rank3_t, rw_t, rw_copied, prep_ok, prep_st, last_ld, var_ok, sd_ok, xn_ok, w_ok, tr_done,
             tr_copied, h_done, h_copied, d_copied) = (sem1(n) for n in (
                "pads", "ld_x", "ld_e", "ld_w", "ld_ffn", "ident_ok", "iota_ok", "dv", "count_ok", "idx_t", "key2_ok",
                "key2_t", "rank2_ok", "rank2_t", "rank3_ok", "rank3_t", "rw_t", "rw_copied", "prep_ok", "prep_st",
                "last_ld", "var_ok", "sd_ok", "xn_ok", "w_ok", "tr_done", "tr_copied", "h_done", "h_copied", "d_copied"))
            row_st = [sem1(f"row_st{u}") for u in range(2)]

            e_rows = lambda a: a[0:gl * P * P].rearrange("(g q e) -> q g e", q=P, e=P)
            n_pads = 4
            n_edge_loads = 7 + gl
            n_ffn_loads = 3 + 2 * NE

            with nc.Block() as block:
                @block.sync
                def _(sp):
                    with nc.allow_non_contiguous_dma(reason="tile borders"):
                        sp.dma_start(dstI[:, 0:gl, :], e_rows(dst)).then_inc(ld_e, 16)
                        sp.dma_start(srcI[:, 0:gl, :], e_rows(src)).then_inc(ld_e, 16)
                        sp.wait_ge(pads, n_pads)
                        for t, a in ((dstI, dst), (srcI, src)):
                            sp.dma_start(t[0:last_full, gl, :],
                                         a[gl * P * P:full_tiles * P].rearrange("(q e) -> q e", e=P)).then_inc(ld_e, 16)
                            sp.dma_start(t[last_full:last_full + 1, gl, 0:rest],
                                         a[full_tiles * P:E].rearrange("(q e) -> q e", q=1)).then_inc(ld_e, 16)
                        col = lambda lo, n: dst[lo:lo + (n - 1) * P + 1:P].rearrange("(q o) -> q o", o=1)
                        sp.dma_start(prevI[1:P, 0:1], col(P - 1, P - 1)).then_inc(ld_e, 16)
                        for g in range(1, gl):
                            sp.dma_start(prevI[:, g:g + 1], col(g * P * P - 1, P)).then_inc(ld_e, 16)
                        sp.dma_start(prevI[0:last_full + 1, gl:G], col(gl * P * P - 1, last_full + 1)).then_inc(ld_e, 16)
                        sp.wait_ge(prep_ok, 1)
                        sp.dma_start(last_d.rearrange("(g q) -> q g", q=P), dstF[:, :, P - 1]).then_inc(last_ld, 16)
                        sp.wait_ge(last_ld, 16)
                        sp.dma_start(lastrow[:, :], last_d[0:NT].partition_broadcast(P)).then_inc(last_ld, 16)
                        sp.wait_ge(prep_ok, 2)
                        sp.dma_start(flag1_d[0:gl * P, :].rearrange("(g q) e -> q g e", q=P),
                                     kF[:, 0:gl].rearrange("q g s e -> q g (s e)")).then_inc(prep_st, 16)
                        sp.dma_start(flag1_d[gl * P:NT, :], kF[0:NT - gl * P, gl].rearrange("q s e -> q (s e)")).then_inc(prep_st, 16)
                        look_v = look_d.rearrange("(g q) e -> q g e", q=P)
                        sp.dma_start(look_v[:, :, 0:P], dstF[:, :, :]).then_inc(prep_st, 16)
                        sp.dma_start(look_v[:, :, P:2 * P], start[:, :, :]).then_inc(prep_st, 16)
                        sp.wait_ge(prep_ok, 3)
                        sp.dma_start(flag2_d, kF2[:, 0].rearrange("g s e -> g (s e)")).then_inc(prep_st, 16)
                        sp.dma_start(flag3_d, kF3[:, 0].rearrange("g s e -> g (s e)")).then_inc(prep_st, 16)
                        sp.dma_start(look_d[0:P - 1, 2 * P:LOOK], rec[1:P, 0, :]).then_inc(prep_st, 16)
                        for g in range(1, G):
                            sp.dma_start(look_d[g * P - 1:(g + 1) * P - 1, 2 * P:LOOK], rec[:, g, :]).then_inc(prep_st, 16)
                        sp.dma_start(look_d[G * P - 1:G * P, 2 * P:LOOK], rec[0:1, 0, :]).then_inc(prep_st, 16)
                        sp.dma_start(part_d[NONE:NONE + 1, :], none_row[:, :]).then_inc(prep_st, 16)

                    def store(u, n):
                        sp.wait_ge(h_copied, 2 * n + u + 1)
                        sp.dma_start(table[bass.ds((2 * n + u) * P, P), :], hrow[:, u, :]).then_inc(row_st[u], 16)
                    with sp.Fori(0, NB // 2) as n:
                        store(0, n)
                        store(1, n)
                    store(0, NB // 2)
                    sp.wait_ge(row_st[0], 16 * (NB // 2 + 1))
                    sp.wait_ge(row_st[1], 16 * (NB // 2))
                    sp.wait_ge(prep_st, 16 * (8 + G))

                @block.gpsimd
                def _(pool):
                    nc.gpsimd.memset(ident[:], 0.0).then_inc(ident_ok, 1)
                    pool.wait_ge(ident_ok, 1)
                    nc.gpsimd.affine_select(out=ident[:], in_=ident[:], compare_op=ALU.not_equal, fill=1.0,
                                            base=0, pattern=[[-1, P]], channel_multiplier=1).then_inc(ident_ok, 1)
                    imp = dict(allow_small_or_imprecise_dtypes=True)
                    nc.gpsimd.iota(nodecol[:], pattern=[[P, NB]], base=0, channel_multiplier=1, **imp).then_inc(iota_ok, 1)
                    nc.gpsimd.iota(tcol[:], pattern=[[P, G]], base=1, channel_multiplier=1, **imp).then_inc(iota_ok, 1)
                    nc.gpsimd.iota(base2[:], pattern=[[P, G]], base=L2BASE, channel_multiplier=0, **imp).then_inc(iota_ok, 1)
                    nc.gpsimd.iota(gi[:], pattern=[[1, P]], base=1, channel_multiplier=0, **imp).then_inc(iota_ok, 1)
                    nc.gpsimd.memset(eps_sb[:], EPS).then_inc(iota_ok, 1)
                    nc.gpsimd.memset(ones[:], 1.0).then_inc(iota_ok, 1)
                    nc.gpsimd.memset(nofirst[:], 1.0).then_inc(iota_ok, 1)
                    nc.gpsimd.memset(none_row[:, 0:ROW], 0.0).then_inc(iota_ok, 1)
                    nc.gpsimd.memset(none_row[:, ROW:WIDE], -BIG).then_inc(iota_ok, 1)
                    pool.wait_ge(iota_ok, 9)
                    nc.gpsimd.memset(nofirst[:, :, 0], 0.0).then_inc(iota_ok, 1)
                    pool.wait_ge(ident_ok, 2)
                    pool.wait_ge(iota_ok, 10)

                @block.vector
                def _(dve):
                    n_dv = [0]

                    def link(ins):
                        n_dv[0] += 1
                        ins.then_inc(dv, 1)
                        dve.wait_ge(dv, n_dv[0])

                    v = nc.vector

                    def runs(key, first_, flags_, rank_, reset):
                        flat = lambda a: a.rearrange("p n e -> p (n e)")
                        link(v.memset(first_[:, :, 0], 1.0))
                        link(v.tensor_tensor(first_[:, :, 1:P], key[:, :, 1:P], key[:, :, 0:P - 1], ALU.not_equal))
                        link(v.tensor_scalar(flags_[:, :, 0, :], first_[:, :, :], -BIG, None, ALU.mult))
                        link(v.memset(flags_[:, :, 1, 0], -BIG))
                        link(v.tensor_scalar(flags_[:, :, 1, 1:P], first_[:, :, P - 1:0:-1], -BIG, None, ALU.mult))
                        link(v.tensor_tensor_scan(flat(rank_), flat(reset), flat(first_), 0.0, ALU.mult, ALU.add))
                        link(v.tensor_scalar(flat(rank_), flat(rank_), -1.0, None, ALU.add))

                    v.memset(dstI[:, gl, :], 8191).then_inc(pads, 1)
                    v.memset(srcI[:, gl, :], 0).then_inc(pads, 1)
                    v.memset(prevI[:, :], -5).then_inc(pads, 1)
                    v.memset(xall[:, NB - 1, :], 0.0).then_inc(pads, 1)
                    dve.wait_ge(ld_e, 16 * n_edge_loads)
                    link(v.tensor_copy(dstF[:, :, :], dstI[:, :, :]))
                    dve.sem_inc(prep_ok, 1)
                    link(v.tensor_copy(srcF[:, :, :], srcI[:, :, :]))
                    link(v.tensor_copy(prevF[:, :], prevI[:, :]))
                    dve.wait_ge(iota_ok, 10)
                    runs(dstF[:, :, :], start[:, :, :], kF[:, :, :, :], rank[:, :, :], nofirst[:, :, :])
                    dve.sem_inc(prep_ok, 1)
                    link(v.tensor_tensor(cont[:, :], dstF[:, :, 0], prevF[:, :], ALU.is_equal))
                    link(v.tensor_tensor(key2[:, :], dstF[:, :, 0], tcol[:, :], ALU.add))
                    link(v.tensor_tensor(key2[:, :], key2[:, :], cont[:, :], ALU.mult))
                    link(v.tensor_tensor(key2[:, :], key2[:, :], tcol[:, :], ALU.subtract))
                    dve.sem_inc(key2_ok, 1)
                    dve.wait_ge(ld_w, 16 * (2 + H))
                    for s in range(2):
                        link(v.tensor_tensor(wprod[:, :, :, :], wraw[:, :, :, :],
                                             attb[:, :, s * DH:(s + 1) * DH].unsqueeze(1).to_broadcast([P, KC, H, DH]), ALU.mult))
                        o = wcat[:, :, 0:ROW].rearrange("p c (h w) -> p c h w", h=H)[:, :, :, DH] if s == 0 else wcat[:, :, ROW:WIDE]
                        link(v.tensor_reduce(o, wprod[:, :, :, :], AX, ALU.add))
                    for k in range(KC):
                        link(v.tensor_copy(wcat[:, k, 0:ROW].rearrange("p (h w) -> p h w", h=H)[:, :, 0:DH], wraw[:, k]))
                    dve.sem_inc(w_ok, 1)
                    dve.wait_ge(idx_t, 3 * G)
                    for j, o in enumerate((rankC, startC, srcC)):
                        for g in range(G):
                            m = j * G + g
                            link(v.tensor_copy(o[:, g * P:(g + 1) * P], bank[m // 4][:, (m % 4) * P:(m % 4 + 1) * P]))
                    dve.wait_ge(key2_t, 2)
                    link(v.tensor_copy(k2r[:, 0, :], bank[6][0:G, 0:P]))
                    link(v.tensor_copy(last2[:, :], bank[6][0:1, P:P + G]))
                    runs(k2r[:, :, :], start2[:, :, :], kF2[:, :, :, :], rank2[:, :, :], nofirst[0:G, 0:1, :])
                    link(v.tensor_scalar(k3r[:, 0, :], gi[:, :], -1.0, None, ALU.mult))
                    link(v.tensor_tensor(eq3[:, 1:G], key2[0:1, 1:G], last2[:, 0:G - 1], ALU.is_equal))
                    link(v.tensor_tensor(last2[:, 1:G], key2[0:1, 1:G], gi[:, 1:G], ALU.add))
                    link(v.tensor_tensor(last2[:, 1:G], last2[:, 1:G], eq3[:, 1:G], ALU.mult))
                    link(v.tensor_tensor(k3r[:, 0, 1:G], last2[:, 1:G], gi[:, 1:G], ALU.subtract))
                    runs(k3r[:, :, :], start3[:, :, :], kF3[:, :, :, :], rank3[:, :, :], nofirst[0:1, 0:1, :])
                    link(v.tensor_copy(rec3[:, 0, :], k3r[:, 0, 1:G + 1]))
                    link(v.tensor_scalar(rec3[:, 1, :], rank3[:, 0, 1:G + 1], float(L3BASE), None, ALU.add))
                    dve.sem_inc(rank2_ok, 1)
                    dve.wait_ge(rank2_t, 1)
                    link(v.tensor_copy(rank2C[:, :], bank[7][:, 0:G]))
                    link(v.tensor_copy(start2C[:, :], bank[7][:, 8:8 + G]))
                    link(v.tensor_copy(rank3C[:, :], bank[7][:, 16:17]))
                    link(v.tensor_copy(start3C[:, :], bank[7][:, 17:18]))
                    link(v.tensor_copy(rec[:, :, 0], dstF[:, :, 0]))
                    link(v.tensor_tensor(rec[:, :, 1], rank2C[:, :], base2[:, :], ALU.add))
                    link(v.tensor_copy(rec[:, :, 2:4], bank[7][:, 24:24 + 2 * G].rearrange("p (s g) -> p g s", s=2)))
                    dve.sem_inc(prep_ok, 1)
                    link(v.tensor_scalar(firstI[:, :], dstF[:, :, 0], float(NB * P - 1), None, ALU.min))
                    dve.wait_ge(rw_t, KC)
                    link(v.tensor_copy(rwT[:, :, :], bank[7][:, 64:64 + KC * NE].rearrange("p (k e) -> p k e", k=KC)))
                    dve.wait_ge(ld_x, 16 * 2)
                    with dve.Fori(0, NB) as b:
                        v.bn_stats(stat[:, bass.ds(b, 1), :].rearrange("p a s -> p (a s)"),
                                   xall[:, bass.ds(b, 1), :].rearrange("p a d -> p (a d)")).then_inc(var_ok, 1)
                    dve.wait_ge(var_ok, NB)
                    link(v.tensor_tensor(mv[:, :, 0], stat[:, :, 1], stat[:, :, 4], ALU.add))
                    link(v.tensor_tensor(mv[:, :, 1], stat[:, :, 1], stat[:, :, 4], ALU.subtract))
                    link(v.tensor_scalar(mv[:, :, 0], mv[:, :, 0], 0.5, None, ALU.mult))
                    link(v.tensor_tensor(mv[:, :, 1], mv[:, :, 1], mv[:, :, 1], ALU.mult))
                    link(v.tensor_tensor(stat[:, :, 2], stat[:, :, 2], stat[:, :, 5], ALU.add))
                    link(v.tensor_scalar(mv[:, :, 1], mv[:, :, 1], 0.25, None, ALU.mult))
                    link(v.scalar_tensor_tensor(mv[:, :, 1], stat[:, :, 2], 1.0 / D, mv[:, :, 1], ALU.mult, ALU.add))
                    dve.sem_inc(var_ok, 1)
                    dve.wait_ge(last_ld, 32)

                    def count(b, u):
                        v.tensor_scalar(junk[:, u, :], lastrow[:, :], nodecol[:, bass.ds(b, 1)], 0.0, ALU.is_lt, ALU.add,
                                        accum_out=cF[:, bass.ds(b, 1)]).then_inc(count_ok, 1)

                    count(0, 0)
                    count(1, 1)
                    with dve.Fori(1, NB // 2) as n:
                        for u in range(2):
                            dve.wait_ge(count_ok, 2 * n + u - 1)
                            count(2 * n + u, u)
                    dve.wait_ge(count_ok, NB - 2)
                    count(NB - 1, 0)
                    dve.wait_ge(count_ok, NB)
                    link(v.tensor_copy(cI[:, :], cF[:, :]))
                    dve.wait_ge(sd_ok, 1)
                    link(v.reciprocal(rstd[:, :], sd[:, :]))

                    def norm(b, u, fresh=False):
                        if not fresh:
                            dve.wait_ge(tr_done, b - 1)
                        xb = xall[:, bass.ds(b, 1), :].rearrange("p a d -> p (a d)")
                        v.tensor_scalar(xn1[:, u, :], xb, mv[:, bass.ds(b, 1), 0], rstd[:, bass.ds(b, 1)],
                                        ALU.subtract, ALU.mult).then_inc(xn_ok, 1)

                    def rows(u, n):
                        dve.wait_ge(h_done, 2 * n + u + 1)
                        if not (isinstance(n, int) and n == 0):
                            dve.wait_ge(row_st[u], 16 * n)
                        v.tensor_copy(hrow[:, u, :], bank[6 + u][:, 0:WIDE]).then_inc(h_copied, 1)
                        v.tensor_copy(dN[:, bass.ds(2 * n + u, 1), :].rearrange("p a h -> p (a h)"),
                                      bank[6 + u][:, ROW:WIDE]).then_inc(d_copied, 1)

                    dve.sem_inc(rw_copied, 1)
                    norm(0, 0, True)
                    norm(1, 1, True)
                    norm(2, 0)
                    rows(0, 0)
                    norm(3, 1)
                    rows(1, 0)
                    with dve.Fori(1, NB // 2 - 1) as n:
                        norm(2 * n + 2, 0)
                        rows(0, n)
                        norm(2 * n + 3, 1)
                        rows(1, n)
                    norm(NB - 1, 0)
                    rows(0, NB // 2 - 1)
                    rows(1, NB // 2 - 1)
                    rows(0, NB // 2)

                @block.tensor
                def _(pe):
                    T = nc.tensor
                    pe.wait_ge(ident_ok, 2)
                    pe.wait_ge(prep_ok, 2)
                    for j, a in enumerate((rank, start, srcF)):
                        for g in range(G):
                            m = j * G + g
                            T.transpose(bank[m // 4][:, (m % 4) * P:(m % 4 + 1) * P], a[:, g, :], ident[:]).then_inc(idx_t, 1)
                    pe.wait_ge(key2_ok, 1)
                    T.transpose(bank[6][0:G, 0:P], key2[:, :], ident[:]).then_inc(key2_t, 1)
                    T.matmul(bank[6][0:1, P:P + G], ident[:, P - 1:P], key2[:, :], start=True, stop=True).then_inc(key2_t, 1)
                    pe.wait_ge(rank2_ok, 1)
                    T.transpose(bank[7][:, 0:G], rank2[:, 0, :], ident[0:G, 0:G])
                    T.transpose(bank[7][:, 8:8 + G], start2[:, 0, :], ident[0:G, 0:G])
                    T.transpose(bank[7][:, 16:17], rank3[:, 0, :], ident[0:1, 0:1])
                    T.transpose(bank[7][:, 17:18], start3[:, 0, :], ident[0:1, 0:1])
                    T.matmul(bank[7][:, 24:24 + 2 * G], ones[:, :], rec3[:, :, :].rearrange("p s g -> p (s g)"),
                             start=True, stop=True).then_inc(rank2_t, 1)
                    pe.wait_ge(prep_ok, 3)
                    pe.wait_ge(ld_ffn, 16 * n_ffn_loads)
                    for k in range(KC):
                        T.transpose(bank[7][:, 64 + k * NE:64 + (k + 1) * NE], rwr[:, k * P:(k + 1) * P], ident[0:NE, 0:NE]).then_inc(rw_t, 1)
                    pe.wait_ge(w_ok, 1)
                    pe.wait_ge(rw_copied, 1)
                    def turn(u, n):
                        pe.wait_ge(xn_ok, 2 * n + u + 1)
                        if not (isinstance(n, int) and n == 0):
                            pe.wait_ge(tr_copied, 2 * n + u - 1)
                        for k in range(KC):
                            t = nc.tensor.transpose(bank[4 + u][:, k * P:(k + 1) * P],
                                                    xn1[:, u, k * P:(k + 1) * P], ident[:])
                        t.then_inc(tr_done, 1)

                    def product(u, n):
                        pe.wait_ge(tr_copied, 2 * n + u + 1)
                        if not (isinstance(n, int) and n == 0):
                            pe.wait_ge(h_copied, 2 * n + u - 1)
                            pe.wait_ge(d_copied, 2 * n + u - 1)
                        for k in range(KC):
                            m = nc.tensor.matmul(bank[6 + u][:, 0:WIDE], xnT[:, u, k, :], wcat[:, k, :], start=k == 0, stop=k == KC - 1)
                        m.then_inc(h_done, 1)

                    turn(0, 0)
                    turn(1, 0)
                    product(0, 0)
                    turn(0, 1)
                    product(1, 0)
                    turn(1, 1)
                    with pe.Fori(1, NB // 2 - 1) as n:
                        product(0, n)
                        turn(0, n + 1)
                        product(1, n)
                        turn(1, n + 1)
                    m = NB // 2 - 1
                    product(0, m)
                    turn(0, m + 1)
                    product(1, m)
                    product(0, m + 1)

                @block.scalar
                def _(act):
                    nc_x = x[0:(NB - 1) * P, :].rearrange("(b p) d -> p b d", p=P)
                    for h in range(H):
                        act.dma_start(wraw[:, :, h, :], W[h].rearrange("(k p) d -> p k d", p=P)).then_inc(ld_w, 16)
                    act.dma_start(attb[:, :, :], attn.partition_broadcast(P)).then_inc(ld_w, 16)
                    act.dma_start(wout_sb[:, :, :], W_out.rearrange("(k p) n -> p k n", p=P)).then_inc(ld_w, 16)
                    act.dma_start(xall[:, 0:NB - 1, :], nc_x).then_inc(ld_x, 16)
                    act.wait_ge(pads, n_pads)
                    act.dma_start(xall[0:TAIL, NB - 1, :], x[(NB - 1) * P:N, :]).then_inc(ld_x, 16)
                    act.dma_start(rwr[:, :], rw).then_inc(ld_ffn, 16)
                    act.dma_start(b2_sb[:, :], b2).then_inc(ld_ffn, 16)
                    with nc.allow_non_contiguous_dma(reason="biases by partition"):
                        act.dma_start(b1_sb[:, :, :].rearrange("p e k -> p (e k)"), b1.rearrange("e (k p) -> p (e k)", p=P)).then_inc(ld_ffn, 16)
                    for e in range(NE):
                        act.dma_start(w1_sb[:, e], w1[e].rearrange("(k p) n -> p k n", p=P)).then_inc(ld_ffn, 16)
                        act.dma_start(w2_sb[:, e], w2[e].rearrange("(k p) n -> p k n", p=P)).then_inc(ld_ffn, 16)
                    act.wait_ge(var_ok, NB + 1)
                    act.wait_ge(iota_ok, 10)
                    nc.scalar.activation(sd[:, :], mv[:, :, 1], ACT.Sqrt, bias=eps_sb[:, 0:1]).then_inc(sd_ok, 1)

                    def copies(u, n):
                        act.wait_ge(tr_done, 2 * n + u + 1)
                        if not (isinstance(n, int) and n == 0):
                            act.wait_ge(h_done, 2 * n + u - 1)
                        nc.scalar.copy(xnT[:, u].rearrange("p k n -> p (k n)"), bank[4 + u][:, 0:KC * P]).then_inc(tr_copied, 1)

                    copies(0, 0)
                    copies(1, 0)
                    copies(0, 1)
                    copies(1, 1)
                    with act.Fori(1, NB // 2 - 1) as n:
                        copies(0, n + 1)
                        copies(1, n + 1)
                    m = NB // 2 - 1
                    copies(0, m + 1)

        with ExitStack() as st:
            def s2(name, shape, dt=F32):
                return st.enter_context(nc.sbuf_tensor(name, shape, dt))

            def sem2(name):
                return st.enter_context(nc.semaphore(name))

            look = s2("look", [P, 2, GB, LOOK])
            lookI = s2("lookI", [P, 2, GB], I32)
            nid = s2("nid", [P, GB])
            junk = s2("junk2", [P, 3, GB, P])
            sums = s2("sums", [P, 3, GB])
            here = s2("here", [P, 3, GB])
            pos = s2("pos", [P, GB])
            offI = s2("offI", [P, 2, GB], I32)
            dS = s2("dS", [P, 2, GB, H])
            fr = s2("fr", [P, G, WIDE])
            keep = s2("keep", [P, G, P])
            fill_done = sem2("fill_done")
            spread = s2("spread", [P, G, P, H])
            filled = s2("filled", [P, G, P, H])
            look_ix, lk, sums_ok, put_ok, zero_ok, zero_st, first_ld, spread_ld, first_ok, fill_ok, fill_t = (
                sem2(n) for n in ("look_ix", "lk", "sums_ok", "put_ok", "zero_ok", "zero_st", "first_ld",
                                  "spread_ld", "first_ok", "fill_ok", "fill_t"))
            looked = [sem2(f"looked{u}") for u in range(2)]
            put = [sem2(f"put{u}") for u in range(2)]
            hold2 = sem2("hold2")
            NOWHERE = 2 * G * P * P
            PAIRS = GROUPS // 2

            with nc.Block() as block:
                @block.sync
                def _(sp):
                    sp.wait_ge(zero_ok, 1)
                    sp.dma_start(start_d.rearrange("(p e) h -> p (e h)", p=P), spread[:, :, :, :].rearrange("p g e h -> p (g e h)")).then_inc(zero_st, 16)
                    sp.wait_ge(put[0], 16 * GB * (PAIRS + 1))
                    sp.wait_ge(put[1], 16 * GB * PAIRS)
                    sp.wait_ge(zero_st, 16)
                    sp.dma_start(spread[:, :, :, :].rearrange("p g e h -> p g (e h)"),
                                 start_d.rearrange("(g q e) h -> q g (e h)", q=P, e=P)).then_inc(spread_ld, 16)
                    sp.wait_ge(spread_ld, 16)

                @block.gpsimd
                def _(pool):
                    def find(u, n):
                        pool.wait_ge(look_ix, 2 * n + u + 1)
                        pool.sem_inc(hold2, 1)
                        for i in range(GB):
                            pool.indirect_dma_start(out=look[:, u, i, :], out_offset=None, in_=look_d[:, :],
                                                    in_offset=bass.IndirectOffsetOnAxis(ap=lookI[:, u, i:i + 1], axis=0)).then_inc(looked[u], 16)

                    def scatter(u, n):
                        pool.wait_ge(put_ok, 2 * n + u + 1)
                        pool.sem_inc(hold2, 1)
                        for i in range(GB):
                            pool.indirect_dma_start(out=start_d[:, :], out_offset=bass.IndirectOffsetOnAxis(ap=offI[:, u, i:i + 1], axis=0),
                                                    in_=dS[:, u, i, :], in_offset=None, bounds_check=G * P * P - 1,
                                                    oob_is_err=False).then_inc(put[u], 16)

                    find(0, 0)
                    find(1, 0)
                    for g in range(G):
                        pool.indirect_dma_start(out=fr[:, g, :], out_offset=None, in_=table[:, :],
                                                in_offset=bass.IndirectOffsetOnAxis(ap=firstI[:, g:g + 1], axis=0)).then_inc(first_ld, 16)
                    pool.wait_ge(zero_st, 16)
                    scatter(0, 0)
                    with pool.Fori(1, PAIRS) as n:
                        find(0, n)
                        scatter(1, n - 1)
                        find(1, n)
                        scatter(0, n)
                    find(0, PAIRS)
                    scatter(1, PAIRS - 1)
                    scatter(0, PAIRS)

                @block.vector
                def _(dve):
                    v = nc.vector
                    LINKS = 17
                    v.memset(spread[:, :, :, :], 0.0).then_inc(zero_ok, 1)

                    def ask(u, n):
                        v.tensor_copy(lookI[:, u, :], cI[:, bass.ds((2 * n + u) * GB, GB)]).then_inc(look_ix, 1)

                    def answer(u, n):
                        g = 2 * n + u
                        b0 = g * GB
                        cnt = [0]

                        def link(ins):
                            cnt[0] += 1
                            ins.then_inc(lk, 1)
                            dve.wait_ge(lk, g * LINKS + cnt[0])

                        link(v.tensor_copy(nid[:, :], nodecol[:, bass.ds(b0, GB)]))
                        dve.wait_ge(looked[u], 16 * GB * (n + 1))
                        for i in range(GB):
                            d_, s_ = look[:, u, i, 0:P], look[:, u, i, P:2 * P]
                            v.tensor_scalar(junk[:, 0, i, :], d_, nid[:, i:i + 1], 0.0, ALU.is_lt, ALU.add, accum_out=sums[:, 0, i:i + 1]).then_inc(sums_ok, 1)
                            v.scalar_tensor_tensor(junk[:, 1, i, :], d_, nid[:, i:i + 1], s_, ALU.is_lt, ALU.mult, accum_out=sums[:, 1, i:i + 1]).then_inc(sums_ok, 1)
                            v.tensor_scalar(junk[:, 2, i, :], d_, nid[:, i:i + 1], 0.0, ALU.is_equal, ALU.add, accum_out=sums[:, 2, i:i + 1]).then_inc(sums_ok, 1)
                        dve.wait_ge(sums_ok, (g + 1) * 3 * GB)
                        link(v.tensor_scalar(here[:, 0, :], sums[:, 2, :], 1.0, None, ALU.min))
                        link(v.tensor_tensor(here[:, 1, :], look[:, u, :, 2 * P], nid[:, :], ALU.is_equal))
                        link(v.tensor_tensor(here[:, 1, :], here[:, 1, :], here[:, 0, :], ALU.mult))
                        link(v.tensor_tensor(here[:, 2, :], look[:, u, :, 2 * P + 2], nid[:, :], ALU.is_equal))
                        link(v.tensor_tensor(here[:, 2, :], here[:, 2, :], here[:, 1, :], ALU.mult))
                        link(v.tensor_scalar(pos[:, :], cF[:, bass.ds(b0, GB)], float(P), None, ALU.mult))
                        link(v.tensor_tensor(sums[:, 0, :], sums[:, 0, :], pos[:, :], ALU.add))
                        link(v.tensor_tensor(sums[:, 1, :], sums[:, 1, :], pos[:, :], ALU.add))
                        for k, a in enumerate((sums[:, 1, :], look[:, u, :, 2 * P + 1], look[:, u, :, 2 * P + 3])):
                            link(v.scalar_tensor_tensor(junk[:, k, 0, 0:GB], a, -float(NONE), here[:, k, :], ALU.add, ALU.mult))
                            link(v.tensor_scalar(rowsN[:, k, bass.ds(b0, GB)], junk[:, k, 0, 0:GB], float(NONE), None, ALU.add))
                        link(v.scalar_tensor_tensor(pos[:, :], sums[:, 0, :], -float(NOWHERE), here[:, 0, :], ALU.add, ALU.mult))
                        assert cnt[0] == LINKS - 1, cnt
                        if not (isinstance(n, int) and n == 0):
                            dve.wait_ge(put[u], 16 * GB * n)
                        link(v.tensor_scalar(offI[:, u, :], pos[:, :], float(NOWHERE), None, ALU.add))
                        v.tensor_copy(dS[:, u, :, :], dN[:, bass.ds(b0, GB), :]).then_inc(put_ok, 1)

                    ask(0, 0)
                    ask(1, 0)
                    answer(0, 0)
                    with dve.Fori(1, PAIRS) as n:
                        ask(0, n)
                        answer(1, n - 1)
                        ask(1, n)
                        answer(0, n)
                    ask(0, PAIRS)
                    answer(1, PAIRS - 1)
                    answer(0, PAIRS)
                    dve.wait_ge(spread_ld, 16)
                    dve.wait_ge(first_ld, 16 * G)
                    v.tensor_copy(spread[:, :, 0, :], fr[:, :, ROW:WIDE]).then_inc(first_ok, 1)
                    link_ = v.tensor_scalar(keep[:, :, :], start[:, :, :], -1.0, 1.0, ALU.mult, ALU.add)
                    link_.then_inc(first_ok, 1)
                    dve.wait_ge(first_ok, 2)
                    flat = lambda a: a.rearrange("p g e -> p (g e)")
                    for h in range(H):
                        v.tensor_tensor_scan(flat(filled[:, :, :, h]), flat(keep[:, :, :]), flat(spread[:, :, :, h]), 0.0,
                                             ALU.mult, ALU.add).then_inc(fill_ok, 1)
                    for h in range(H):
                        for g in range(G):
                            m = h * G + g
                            if m % 4 == 0:
                                dve.wait_ge(fill_t, m // 4 + 1)
                            n_ = min(P, NT - g * P)
                            v.tensor_copy(De[:, g * P:g * P + n_, h], bank[m // 4 % 8][:, (m % 4) * P:(m % 4) * P + n_]).then_inc(fill_done, 1)
                    dve.wait_ge(fill_done, H * G)

                @block.tensor
                def _(pe):
                    for h in range(H):
                        pe.wait_ge(fill_ok, h + 1)
                        for g in range(G):
                            m = h * G + g
                            t = nc.tensor.transpose(bank[m // 4 % 8][:, (m % 4) * P:(m % 4 + 1) * P], filled[:, g, :, h], ident[:])
                            if m % 4 == 3:
                                t.then_inc(fill_t, 1)
        pre.close()

        with ExitStack() as st:
            def s3(name, shape, dt=F32):
                return st.enter_context(nc.sbuf_tensor(name, shape, dt))

            def sem3(name):
                return st.enter_context(nc.semaphore(name))

            ring = s3("ring", [P, RING * BT, WIDE])
            ring4 = ring[:, :, 0:ROW].rearrange("p k (h w) -> p k h w", h=H)
            idx = s3("idx", [P, RING, BT], I32)
            flags = s3("flags", [ZW, RING, 2, P])
            ranks = s3("ranks", [P, P])
            z = s3("z", [P, ZW])
            eC = s3("eC", [P, ZW])
            f1 = s3("f1", [ZW, P])
            r1 = s3("r1", [ZW, P])
            rho = s3("rho", [ZW, P])
            arg = s3("arg", [P, ZW])
            w23 = s3("w23", [P, ZW])
            oh = s3("oh", [P, RING, BT, P])
            stage = s3("stage", [P, 2, 4, WIDE])
            S = {n: sem3("b_" + n) for n in "z e oh eT f1 r1 rho rc ms arg al msg agg ev setup hold_pool hold_pe hold_act hold_sp".split()}
            idx_ld = [sem3(f"idx_ld{r}") for r in range(RING)]
            flag_ld = [sem3(f"flag_ld{r}") for r in range(RING)]
            gathered = [sem3(f"gathered{r}") for r in range(RING)]
            stored = [sem3(f"stored{r}") for r in range(2)]
            upper_ld = sem3("upper_ld")
            upper_zero = sem3("upper_zero")

            ROUNDS = NBAT // RING
            assert NBAT == ROUNDS * RING + 1 and BT == 16
            QUADS = BT // 4
            UPPER = [(G, flag2_d, rank2C, start2C, L2BASE), (1, flag3_d, rank3C, start3C, L3BASE)]
            quads = lambda tiles: -(-tiles // 4)
            before = [(NT, NBAT * QUADS), (NT + G, NBAT * QUADS + quads(G))]

            with nc.Block() as block:
                @block.sync
                def _(sp):
                    def fetch(r, n):
                        t0 = (RING * n + r) * BT
                        if not (isinstance(n, int) and n == 0):
                            sp.wait_ge(gathered[r], 16 * BT * n)
                            sp.sem_inc(S["hold_sp"], 1)
                            sp.wait_ge(S["rho"], RING * n + r - 2)
                            sp.sem_inc(S["hold_sp"], 1)
                        sp.dma_start(idx[:, r, :], srcC[:, bass.ds(t0, BT)]).then_inc(idx_ld[r], 16)
                        for s in range(2):
                            sp.dma_start(flags[:, r, s, :],
                                         flag1_d[bass.ds(t0, BT), s * P:(s + 1) * P].unsqueeze(1).to_broadcast([BT, H, P])).then_inc(flag_ld[r], 16)

                    def store(r, n):
                        beta = RING * n + r
                        for q in range(QUADS):
                            sp.wait_ge(S["ev"], beta * BT + 4 * q + 4)
                            sp.sem_inc(S["hold_sp"], 1)
                            sp.dma_start(part_d[bass.ds((beta * BT + 4 * q) * P, 4 * P), :].rearrange("(k s) w -> s k w", k=4),
                                         stage[:, q % 2]).then_inc(stored[q % 2], 16)

                    fetch(0, 0)
                    fetch(1, 0)
                    fetch(2, 0)
                    store(0, 0)
                    fetch(0, 1)
                    store(1, 0)
                    fetch(1, 1)
                    store(2, 0)
                    with sp.Fori(1, ROUNDS - 1) as n:
                        fetch(2, n)
                        store(0, n)
                        fetch(0, n + 1)
                        store(1, n)
                        fetch(1, n + 1)
                        store(2, n)
                    m = ROUNDS - 1
                    fetch(2, m)
                    store(0, m)
                    fetch(0, m + 1)
                    store(1, m)
                    store(2, m)
                    store(0, m + 1)
                    n_st = [NBAT * QUADS // 2] * 2
                    sp.wait_ge(S["rho"], NBAT)
                    for lv, (tiles, flag_d, _, _, base) in enumerate(UPPER):
                        for s in range(2):
                            sp.dma_start(flags[0:tiles * H, 1 + lv, s, :],
                                         flag_d[:, s * P:(s + 1) * P].unsqueeze(1).to_broadcast([tiles, H, P])).then_inc(upper_ld, 16)
                    sp.wait_ge(upper_zero, 1)
                    for u in range(2):
                        sp.wait_ge(stored[u], 16 * n_st[u])
                    tiles_below = part_d[0:NT * P, :].rearrange("(t s) w -> t s w", s=P)
                    sp.dma_start(ring[:, BT:BT + gl, :], tiles_below[0:gl * P, 0, :].rearrange("(g q) w -> q g w", q=P)).then_inc(upper_ld, 16)
                    sp.dma_start(ring[0:NT - gl * P, BT + gl, :], tiles_below[gl * P:NT, 0, :]).then_inc(upper_ld, 16)

                    def store_upper(lv):
                        tiles, _, _, _, base = UPPER[lv]
                        done = before[lv][0]
                        for q in range(quads(tiles)):
                            k = min(4, tiles - 4 * q)
                            sp.wait_ge(S["ev"], done + 4 * q + k)
                            u = q % 2
                            sp.dma_start(part_d[base + 4 * q * P:base + (4 * q + k) * P, :].rearrange("(k s) w -> s k w", k=k),
                                         stage[:, u, 0:k]).then_inc(stored[u], 16)
                            n_st[u] += 1
                        for u in range(2):
                            sp.wait_ge(stored[u], 16 * n_st[u])

                    store_upper(0)
                    sp.dma_start(ring[0:G, 2 * BT, :], part_d[L2BASE:L2BASE + G * P, :].rearrange("(t s) w -> t s w", s=P)[:, 0, :]).then_inc(upper_ld, 16)
                    store_upper(1)

                @block.gpsimd
                def _(pool):
                    nc.gpsimd.iota(ranks[:], pattern=[[1, P]], base=0, channel_multiplier=0,
                                   allow_small_or_imprecise_dtypes=True).then_inc(S["setup"], 1)

                    def gather(r, n):
                        pool.wait_ge(idx_ld[r], 16 * (n + 1))
                        if not (isinstance(n, int) and n == 0):
                            pool.wait_ge(S["agg"], BT * (RING * n + r - 2))
                        pool.sem_inc(S["hold_pool"], 1)
                        for k in range(BT):
                            pool.indirect_dma_start(out=ring[:, r * BT + k, :], out_offset=None, in_=table[:, :],
                                                    in_offset=bass.IndirectOffsetOnAxis(ap=idx[:, r, k:k + 1], axis=0)).then_inc(gathered[r], 16)
                    for r in range(RING):
                        gather(r, 0)
                    with pool.Fori(1, ROUNDS) as n:
                        for r in range(RING):
                            gather(r, n)
                    gather(0, ROUNDS)

                @block.vector
                def _(dve):
                    v = nc.vector
                    dve.wait_ge(S["setup"], 1)

                    def segment_max(count, rows_, eT, kf, kr):
                        dve.wait_ge(S["eT"], count)
                        v.tensor_tensor_scan(f1[0:rows_, :], kf, eT, -BIG, ALU.add, ALU.max).then_inc(S["f1"], 1)
                        v.tensor_tensor_scan(r1[0:rows_, ::-1], kr, eT[:, ::-1], -BIG, ALU.add, ALU.max).then_inc(S["r1"], 1)
                        dve.wait_ge(S["f1"], count)
                        dve.wait_ge(S["r1"], count)
                        v.tensor_tensor(rho[0:rows_, :], f1[0:rows_, :], r1[0:rows_, :], ALU.max).then_inc(S["rho"], 1)

                    def batch(r, n):
                        beta = RING * n + r
                        t0 = beta * BT
                        k0, k1 = r * BT, (r + 1) * BT
                        dve.wait_ge(gathered[r], 16 * BT * (n + 1))
                        v.tensor_tensor(z[:, :].rearrange("p (k h) -> p k h", h=H), ring4[:, k0:k1, :, DH],
                                        De[:, bass.ds(t0, BT), :], ALU.add).then_inc(S["z"], 1)
                        dve.wait_ge(S["z"], beta + 1)
                        v.scalar_tensor_tensor(eC[:, :], z[:, :], 0.2, z[:, :], ALU.mult, ALU.max).then_inc(S["e"], 1)
                        if not (isinstance(n, int) and n == 0):
                            dve.wait_ge(S["agg"], BT * (beta - 2))
                        v.tensor_tensor(oh[:, r, :, :], ranks[:, :].unsqueeze(1).to_broadcast([P, BT, P]),
                                        rankC[:, bass.ds(t0, BT)].unsqueeze(2).to_broadcast([P, BT, P]), ALU.is_equal).then_inc(S["oh"], 1)
                        dve.wait_ge(flag_ld[r], 32 * (n + 1))
                        segment_max(beta + 1, ZW, bank[4][0:ZW, 0:P], flags[:, r, 0, :], flags[:, r, 1, :])
                        dve.wait_ge(S["rc"], beta + 1)
                        rhoT = bank[5][:, 0:ZW].rearrange("p (k h) -> p k h", h=H)
                        v.tensor_tensor(arg[:, :], eC[:, :], bank[5][:, 0:ZW], ALU.subtract).then_inc(S["arg"], 1)
                        v.tensor_tensor(ring[:, k0:k1, ROW:WIDE], rhoT,
                                        startC[:, bass.ds(t0, BT)].unsqueeze(2).to_broadcast([P, BT, H]), ALU.mult).then_inc(S["ms"], 1)
                        dve.wait_ge(S["al"], beta + 1)
                        for q in range(QUADS):
                            m = ring4[:, k0 + 4 * q:k0 + 4 * q + 4, :, 0:DH]
                            v.tensor_tensor(m, m, ring4[:, k0 + 4 * q:k0 + 4 * q + 4, :, DH:HW].to_broadcast([P, 4, H, DH]),
                                            ALU.mult).then_inc(S["msg"], 1)

                    for r in range(RING):
                        batch(r, 0)
                    with dve.Fori(1, ROUNDS) as n:
                        for r in range(RING):
                            batch(r, n)
                    batch(0, ROUNDS)

                    dve.wait_ge(S["agg"], NT)
                    v.memset(ring[:, BT:3 * BT, :], 0.0).then_inc(upper_zero, 1)
                    for lv, (tiles, _, rank_, start_, _) in enumerate(UPPER):
                        c_ = NBAT + lv + 1
                        k0 = (1 + lv) * BT
                        w = tiles * H
                        dve.wait_ge(upper_ld, 16 * (6 + lv))
                        v.tensor_copy(eC[:, 0:w].rearrange("p (k h) -> p k h", h=H), ring[:, k0:k0 + tiles, ROW:WIDE]).then_inc(S["e"], 1)
                        v.tensor_tensor(oh[:, 1 + lv, 0:tiles, :], ranks[:, :].unsqueeze(1).to_broadcast([P, tiles, P]),
                                        rank_[:, :].unsqueeze(2).to_broadcast([P, tiles, P]), ALU.is_equal).then_inc(S["oh"], 1)
                        segment_max(c_, w, bank[4][0:w, 0:P], flags[0:w, 1 + lv, 0, :], flags[0:w, 1 + lv, 1, :])
                        dve.wait_ge(S["rc"], c_)
                        v.tensor_tensor(arg[:, 0:w], eC[:, 0:w], bank[5][:, 0:w], ALU.subtract).then_inc(S["arg"], 1)
                        v.tensor_tensor(ring[:, k0:k0 + tiles, ROW:WIDE], bank[5][:, 0:w].rearrange("p (k h) -> p k h", h=H),
                                        start_[:, :].unsqueeze(2).to_broadcast([P, tiles, H]), ALU.mult).then_inc(S["ms"], 1)
                        dve.wait_ge(S["al"], c_)
                        for q in range(quads(tiles)):
                            k = min(4, tiles - 4 * q)
                            m = ring4[:, k0 + 4 * q:k0 + 4 * q + k, :, :]
                            v.tensor_tensor(m, m, w23[:, 16 * q:16 * q + 4 * k].rearrange("p (k h) -> p k h", h=H).unsqueeze(3).to_broadcast([P, k, H, HW]),
                                            ALU.mult).then_inc(S["msg"], 1)

                @block.tensor
                def _(pe):
                    T = nc.tensor

                    def turns(count, w, hold):
                        pe.wait_ge(S["e"], count)
                        if hold:
                            pe.sem_inc(S["hold_pe"], 1)
                        T.transpose(bank[4][0:w, 0:P], eC[:, 0:w], ident[:]).then_inc(S["eT"], 1)
                        pe.wait_ge(S["rho"], count)
                        if hold:
                            pe.sem_inc(S["hold_pe"], 1)
                        T.transpose(bank[5][:, 0:w], rho[0:w, :], ident[0:w, 0:w]).then_inc(S["rc"], 1)

                    def sums(r, tiles, n_agg, n_msg, fresh):
                        for k in range(tiles):
                            if k % 4 == 0:
                                pe.wait_ge(S["msg"], n_msg + k // 4 + 1)
                            if not (fresh and k < 4):
                                pe.wait_ge(S["ev"], n_agg + k - 3)
                            T.matmul(bank[k % 4][:, 0:WIDE], oh[:, r, k, :], ring[:, r * BT + k, :], start=True, stop=True).then_inc(S["agg"], 1)

                    def batch(r, n):
                        beta = RING * n + r
                        turns(beta + 1, ZW, True)
                        sums(r, BT, beta * BT, beta * QUADS, isinstance(n, int) and n == 0 and r == 0)

                    for r in range(RING):
                        batch(r, 0)
                    with pe.Fori(1, ROUNDS) as n:
                        for r in range(RING):
                            batch(r, n)
                    batch(0, ROUNDS)
                    for lv, (tiles, _, _, _, _) in enumerate(UPPER):
                        turns(NBAT + lv + 1, tiles * H, False)
                        sums(1 + lv, tiles, before[lv][0], before[lv][1], False)

                @block.scalar
                def _(act):
                    A = nc.scalar

                    def evacuate(k, done, quad_uses):
                        act.wait_ge(S["agg"], done + k + 1)
                        if k % 4 == 0 and quad_uses is not None:
                            act.wait_ge(stored[k // 4 % 2], 16 * quad_uses)
                        A.copy(stage[:, k // 4 % 2, k % 4, :], bank[k % 4][:, 0:WIDE]).then_inc(S["ev"], 1)

                    def batch(r, n):
                        beta = RING * n + r
                        act.wait_ge(S["arg"], beta + 1)
                        A.activation(ring4[:, r * BT:(r + 1) * BT, :, DH], arg[:, :].rearrange("p (k h) -> p k h", h=H), ACT.Exp).then_inc(S["al"], 1)
                        first = isinstance(n, int) and n == 0 and r == 0
                        for k in range(BT):
                            evacuate(k, beta * BT, None if first and k < 8 else 2 * beta + k // 8)

                    for r in range(RING):
                        batch(r, 0)
                    with act.Fori(1, ROUNDS) as n:
                        for r in range(RING):
                            batch(r, n)
                    batch(0, ROUNDS)
                    uses = [NBAT * QUADS // 2] * 2
                    for lv, (tiles, _, _, _, _) in enumerate(UPPER):
                        act.wait_ge(S["arg"], NBAT + lv + 1)
                        A.activation(w23[:, 0:tiles * H], arg[:, 0:tiles * H], ACT.Exp).then_inc(S["al"], 1)
                        for k in range(tiles):
                            evacuate(k, before[lv][0], uses[k // 4 % 2])
                        for q in range(quads(tiles)):
                            uses[q % 2] += 1

        with ExitStack() as st:
            def s4(name, shape, dt=F32):
                return st.enter_context(nc.sbuf_tensor(name, shape, dt))

            xg = s4("xg", [P, 2, GB, D])
            x1 = s4("x1", [P, GB, D])
            xn = s4("xn", [P, GB, D])
            y = s4("y", [P, 2, GB, D])
            on = s4("on", [P, GB, D])
            oT = s4("oT", [P, 2, KC, P])
            xnT = s4("xnT4", [P, KC, GB * P])
            hT = s4("hT", [P, 2, KC, 512])
            pa = s4("pa", [P, 2, 3, GB, WIDE])
            rowI = s4("rowI", [P, 2, 3, GB], I32)
            mx = s4("mx", [P, GB, H])
            wl = s4("wl", [P, 3, GB, H])
            den = s4("den", [P, GB, H])
            rden = s4("rden", [P, GB, H])
            stat = s4("stat4", [P, GB, 6])
            mv = s4("mv4", [P, GB, 2])
            sd = s4("sd4", [P, GB])
            rstd = s4("rstd4", [P, GB])
            lg = s4("lg", [P, GB, NE])
            top = s4("top", [P, GB, 8])
            topi = s4("topi", [P, GB, 8], U32)
            topf = s4("topf", [P, GB, 2])
            ex = s4("ex", [P, GB, NE + 2])
            dif = s4("dif", [P, GB, NE + 2])
            sm = s4("sm", [P, GB])
            rsm = s4("rsm", [P, GB])
            pr = s4("pr", [P, GB, 2])
            ps = s4("ps", [P, GB])
            rps = s4("rps", [P, GB])
            wt = s4("wt", [P, GB, 2])
            cmb = s4("cmb", [P, GB, NE])
            cmb2 = s4("cmb2", [P, GB, NE])
            cT = s4("cT", [NE, GB, P])
            iota8 = s4("iota8", [P, NE])
            S = {n: st.enter_context(nc.semaphore("f_" + n)) for n in
                 "t1 t1c o g x1 stats sd xn t2 t2c lg cmb ct ctc yb y0 h1 act y2 yacc link iota last stp hold ask wexp hold_pool".split()}
            fetched = [st.enter_context(nc.semaphore(f"fetched{r}")) for r in range(2)]
            x_ld = [st.enter_context(nc.semaphore(f"x_ld{r}")) for r in range(2)]
            y_st = [st.enter_context(nc.semaphore(f"y_st{r}")) for r in range(2)]
            HALF = [(0, 4), (4, 3)]
            NMM = NE * len(HALF)
            LINKS = 36

            with nc.Block() as block:
                @block.sync
                def _(sp):
                    def load(u, n, rows_last=P):
                        g = 2 * n + u
                        if not (isinstance(n, int) and n == 0):
                            sp.wait_ge(S["x1"], (g - 1) * GB)
                        r0_ = g * GB * P
                        k = GB if rows_last == P else GB - 1
                        sp.dma_start(xg[:, u, 0:k, :], x[bass.ds(r0_, k * P), :].rearrange("(b p) d -> p b d", p=P)).then_inc(x_ld[u], 16)
                        if rows_last != P:
                            sp.dma_start(xg[0:rows_last, u, GB - 1, :], x[r0_ + k * P:N, :]).then_inc(x_ld[u], 16)

                    def store(u, n, rows_last=P):
                        g = 2 * n + u
                        sp.wait_ge(S["last"], g + 1)
                        r0_ = g * GB * P
                        k = GB if rows_last == P else GB - 1
                        sp.dma_start(out[bass.ds(r0_, k * P), :].rearrange("(b p) d -> p b d", p=P), y[:, u, 0:k, :]).then_inc(y_st[u], 16)
                        if rows_last != P:
                            sp.dma_start(out[r0_ + k * P:N, :], y[0:rows_last, u, GB - 1, :]).then_inc(y_st[u], 16)

                    pairs = GROUPS // 2
                    load(0, 0)
                    load(1, 0)
                    with sp.Fori(1, pairs) as n:
                        load(0, n)
                        store(0, n - 1)
                        load(1, n)
                        store(1, n - 1)
                    load(0, pairs, TAIL)
                    store(0, pairs - 1)
                    store(1, pairs - 1)
                    store(0, pairs, TAIL)
                    sp.wait_ge(y_st[0], 16 * (pairs + 2))
                    sp.wait_ge(y_st[1], 16 * pairs)

                @block.gpsimd
                def _(pool):
                    def fetch(u, n):
                        pool.wait_ge(S["ask"], 2 * n + u + 1)
                        pool.sem_inc(S["hold_pool"], 1)
                        for k in range(3):
                            for i in range(GB):
                                pool.indirect_dma_start(out=pa[:, u, k, i, :], out_offset=None, in_=part_d[:, :],
                                                        in_offset=bass.IndirectOffsetOnAxis(ap=rowI[:, u, k, i:i + 1], axis=0)).then_inc(fetched[u], 16)
                    nc.gpsimd.iota(iota8[:], pattern=[[1, NE]], base=0, channel_multiplier=0,
                                   allow_small_or_imprecise_dtypes=True).then_inc(S["iota"], 1)
                    pool.wait_ge(S["iota"], 1)
                    with pool.Fori(0, GROUPS // 2) as n:
                        fetch(0, n)
                        fetch(1, n)
                    fetch(0, GROUPS // 2)

                @block.vector
                def _(dve):
                    v = nc.vector
                    dve.wait_ge(S["iota"], 1)

                    def ask(u, n):
                        v.tensor_copy(rowI[:, u, :, :], rowsN[:, :, bass.ds((2 * n + u) * GB, GB)]).then_inc(S["ask"], 1)

                    ask(0, 0)
                    ask(1, 0)

                    def group(u, n, last=False, ask_next=True):
                        g = 2 * n + u
                        count = [0]

                        def link(ins):
                            count[0] += 1
                            ins.then_inc(S["link"], 1)
                            dve.wait_ge(S["link"], g * LINKS + count[0])

                        dve.wait_ge(fetched[u], 16 * 3 * GB * (n + 1))
                        lm = [pa[:, u, k, :, ROW:WIDE] for k in range(3)]
                        lv = [pa[:, u, k, :, 0:ROW].rearrange("p b (h w) -> p b h w", h=H) for k in range(3)]
                        link(v.tensor_tensor(mx[:, :, :], lm[0], lm[1], ALU.max))
                        link(v.tensor_tensor(mx[:, :, :], mx[:, :, :], lm[2], ALU.max))
                        for k in range(3):
                            link(v.tensor_tensor(wl[:, k], lm[k], mx[:, :, :], ALU.subtract))
                        dve.wait_ge(S["wexp"], g + 1)
                        for k in range(3):
                            link(v.tensor_tensor(lv[k], lv[k], wl[:, k].unsqueeze(3).to_broadcast([P, GB, H, HW]), ALU.mult))
                        for k in range(1, 3):
                            link(v.tensor_tensor(pa[:, u, 0, :, 0:ROW], pa[:, u, 0, :, 0:ROW], pa[:, u, k, :, 0:ROW], ALU.add))
                        link(v.tensor_scalar(den[:, :, :], lv[0][:, :, :, DH], 1e-8, None, ALU.add))
                        link(v.reciprocal(rden[:, :, :], den[:, :, :]))
                        v.tensor_tensor(on[:, :, :].rearrange("p b (h w) -> p b h w", h=H), lv[0][:, :, :, 0:DH],
                                        rden[:, :, :].unsqueeze(3).to_broadcast([P, GB, H, DH]), ALU.mult).then_inc(S["o"], 1)
                        dve.wait_ge(S["o"], g + 1)
                        if ask_next:
                            ask(u, n + 1)
                        dve.wait_ge(x_ld[u], 16 * (n + 1) + (16 if last else 0))
                        for i in range(GB):
                            dve.wait_ge(S["g"], g * GB + i + 1)
                            v.tensor_tensor(x1[:, i, :], xg[:, u, i, :], bank[2 + i % 2][:, 0:D], ALU.add).then_inc(S["x1"], 1)
                            dve.wait_ge(S["x1"], g * GB + i + 1)
                            v.bn_stats(stat[:, i, :], x1[:, i, :]).then_inc(S["stats"], 1)
                        dve.wait_ge(S["stats"], (g + 1) * GB)
                        link(v.tensor_tensor(mv[:, :, 0], stat[:, :, 1], stat[:, :, 4], ALU.add))
                        link(v.tensor_tensor(mv[:, :, 1], stat[:, :, 1], stat[:, :, 4], ALU.subtract))
                        link(v.tensor_scalar(mv[:, :, 0], mv[:, :, 0], 0.5, None, ALU.mult))
                        link(v.tensor_tensor(mv[:, :, 1], mv[:, :, 1], mv[:, :, 1], ALU.mult))
                        link(v.tensor_tensor(stat[:, :, 2], stat[:, :, 2], stat[:, :, 5], ALU.add))
                        link(v.tensor_scalar(mv[:, :, 1], mv[:, :, 1], 0.25, None, ALU.mult))
                        link(v.scalar_tensor_tensor(mv[:, :, 1], stat[:, :, 2], 1.0 / D, mv[:, :, 1], ALU.mult, ALU.add))
                        dve.wait_ge(S["sd"], g + 1)
                        link(v.reciprocal(rstd[:, :], sd[:, :]))
                        for i in range(GB):
                            v.tensor_scalar(xn[:, i, :], x1[:, i, :], mv[:, i, 0:1], rstd[:, i:i + 1], ALU.subtract, ALU.mult).then_inc(S["xn"], 1)
                        dve.wait_ge(S["lg"], g + 1)
                        link(v.tensor_copy(lg[:, :, :], bank[2][:, 0:GB * NE].rearrange("p (b e) -> p b e", b=GB)))
                        dve.sem_inc(S["hold"], 1)
                        for i in range(GB):
                            t = v.max(top[:, i, :], lg[:, i, :])
                            if i < GB - 1:
                                t.then_inc(S["cmb"], 1)
                        link(t)
                        dve.wait_ge(S["cmb"], g * (2 * GB - 1) + GB - 1)
                        dve.sem_inc(S["hold"], 1)
                        for i in range(GB):
                            v.max_index(topi[:, i, :], top[:, i, :], lg[:, i, :]).then_inc(S["cmb"], 1)
                        dve.wait_ge(S["cmb"], (g + 1) * (2 * GB - 1))
                        link(v.tensor_copy(topf[:, :, :], topi[:, :, 0:2]))
                        link(v.tensor_tensor(dif[:, :, 0:NE], lg[:, :, :], top[:, :, 0:1].to_broadcast([P, GB, NE]), ALU.subtract))
                        link(v.tensor_tensor(dif[:, :, NE:NE + 2], top[:, :, 0:2], top[:, :, 0:1].to_broadcast([P, GB, 2]), ALU.subtract))
                        dve.wait_ge(S["y0"], g + 1)
                        link(v.tensor_reduce(sm[:, :], ex[:, :, 0:NE], AX, ALU.add))
                        link(v.reciprocal(rsm[:, :], sm[:, :]))
                        link(v.tensor_tensor(pr[:, :, :], ex[:, :, NE:NE + 2], rsm[:, :].unsqueeze(2).to_broadcast([P, GB, 2]), ALU.mult))
                        link(v.tensor_reduce(ps[:, :], pr[:, :, :], AX, ALU.add))
                        link(v.tensor_scalar(ps[:, :], ps[:, :], 1e-12, None, ALU.max))
                        link(v.reciprocal(rps[:, :], ps[:, :]))
                        link(v.tensor_tensor(wt[:, :, :], pr[:, :, :], rps[:, :].unsqueeze(2).to_broadcast([P, GB, 2]), ALU.mult))
                        for k, o in ((0, cmb), (1, cmb2)):
                            link(v.tensor_tensor(o[:, :, :], iota8[:, :].unsqueeze(1).to_broadcast([P, GB, NE]),
                                                 topf[:, :, k:k + 1].to_broadcast([P, GB, NE]), ALU.is_equal))
                            link(v.tensor_tensor(o[:, :, :], o[:, :, :], wt[:, :, k:k + 1].to_broadcast([P, GB, NE]), ALU.mult))
                        ins = v.tensor_tensor(cmb[:, :, :], cmb[:, :, :], cmb2[:, :, :], ALU.add)
                        ins.then_inc(S["ct"], 1)
                        assert count[0] == LINKS, count
                        dve.wait_ge(S["ct"], g + 1)
                        if not (isinstance(n, int) and n == 0):
                            dve.wait_ge(y_st[u], 16 * n)
                        v.tensor_tensor(y[:, u], x1[:, :, :], xn[:, :, :], ALU.add).then_inc(S["yacc"], 1)
                        adds = 1 + GB + NE * GB
                        dve.wait_ge(S["yacc"], g * adds + 1)
                        for i in range(GB):
                            dve.wait_ge(S["yb"], g * GB + i + 1)
                            v.tensor_tensor(y[:, u, i, :], y[:, u, i, :], bank[2 + i % 2][:, 0:D], ALU.add).then_inc(S["yacc"], 1)
                        m = 0
                        for e in range(NE):
                            for h0, hn in HALF:
                                for i in range(h0, h0 + hn):
                                    dve.wait_ge(S["y2"], g * NE * GB + m + 1)
                                    dve.wait_ge(S["yacc"], g * adds + 1 + m + 1)
                                    t = v.scalar_tensor_tensor(y[:, u, i, :], bank[6 + m % 2][:, 0:D], cmb[:, i, e:e + 1], y[:, u, i, :],
                                                               ALU.mult, ALU.add)
                                    t.then_inc(S["yacc"], 1)
                                    m += 1
                        dve.wait_ge(S["yacc"], (g + 1) * adds)
                        dve.sem_inc(S["last"], 1)

                    pairs = GROUPS // 2
                    group(0, 0)
                    group(1, 0)
                    with dve.Fori(1, pairs - 1) as n:
                        group(0, n)
                        group(1, n)
                    group(0, pairs - 1)
                    group(1, pairs - 1, ask_next=False)
                    group(0, pairs, True, ask_next=False)

                @block.tensor
                def _(pe):
                    T = nc.tensor
                    pe.sem_inc(S["t2c"], 2)

                    def group(u, n):
                        g = 2 * n + u
                        first = isinstance(n, int) and n == 0 and u == 0
                        pe.wait_ge(S["o"], g + 1)

                        def turn(i, src_, sem_):
                            for k in range(KC):
                                t = T.transpose(bank[i % 2][:, k * P:(k + 1) * P], src_[:, i, k * P:(k + 1) * P], ident[:])
                            t.then_inc(S[sem_], 1)

                        def project(i):
                            pe.wait_ge(S["t1c"], g * GB + i + 1)
                            if i >= 2:
                                pe.wait_ge(S["x1"], g * GB + i - 1)
                            for k in range(KC):
                                t = T.matmul(bank[2 + i % 2][:, 0:D], oT[:, i % 2, k, :], wout_sb[:, k, :], start=k == 0, stop=k == KC - 1)
                            t.then_inc(S["g"], 1)

                        turn(0, on, "t1")
                        for i in range(1, GB):
                            if i >= 2:
                                pe.wait_ge(S["t1c"], g * GB + i - 1)
                            turn(i, on, "t1")
                            project(i - 1)
                        project(GB - 1)
                        for i in range(GB):
                            pe.wait_ge(S["xn"], g * GB + i + 1)
                            if i < 2:
                                pe.wait_ge(S["t1c"], (g + 1) * GB)
                            else:
                                pe.wait_ge(S["t2c"], g * GB + i - 1 + 2)
                            turn(i, xn, "t2")
                        pe.wait_ge(S["t2c"], (g + 1) * GB + 2)
                        for i in range(GB):
                            for k in range(KC):
                                t = T.matmul(bank[2][:, i * NE:(i + 1) * NE], xnT[:, k, i * P:(i + 1) * P], rwT[:, k, :],
                                             start=k == 0, stop=k == KC - 1)
                        t.then_inc(S["lg"], 1)

                        def hidden(e, q):
                            h0, hn = HALF[q]
                            m = e * 2 + q
                            for f in range(KC):
                                if not (m == 0 and first):
                                    pe.wait_ge(S["act"], (g * NMM + m) * KC + f - 1)  if not (m == 0) else pe.wait_ge(S["act"], (g * NMM) * KC)
                                for k in range(KC):
                                    t = T.matmul(bank[4 + f][:, 0:hn * P], w1_sb[:, e, k, f * P:(f + 1) * P],
                                                 xnT[:, k, h0 * P:(h0 + hn) * P], start=k == 0, stop=k == KC - 1)
                                t.then_inc(S["h1"], 1)

                        cnt = [0]

                        def output(e, q):
                            h0, hn = HALF[q]
                            m = e * 2 + q
                            pe.wait_ge(S["act"], (g * NMM + m + 1) * KC)
                            for i in range(h0, h0 + hn):
                                a = cnt[0]
                                if a >= 2:
                                    pe.wait_ge(S["yacc"], g * (1 + GB + NE * GB) + 1 + GB + a - 1)
                                for f in range(KC):
                                    t = T.matmul(bank[6 + a % 2][:, 0:D], hT[:, q, f, (i - h0) * P:(i - h0 + 1) * P], w2_sb[:, e, f, :],
                                                 start=f == 0, stop=f == KC - 1)
                                t.then_inc(S["y2"], 1)
                                cnt[0] += 1

                        hidden(0, 0)
                        pe.wait_ge(S["ct"], g + 1)
                        for i in range(GB):
                            if i >= 2:
                                pe.wait_ge(S["ctc"], g * GB + i - 1)
                            T.transpose(bank[i % 2][0:NE, 0:P], cmb[:, i, :], ident[:]).then_inc(S["stp"], 1)
                        for i in range(GB):
                            pe.wait_ge(S["ctc"], g * GB + i + 1)
                            if i >= 2:
                                pe.wait_ge(S["yacc"], g * (1 + GB + NE * GB) + 1 + i - 1)
                            T.matmul(bank[2 + i % 2][:, 0:D], cT[:, i, :], b2_sb[:, :], start=True, stop=True).then_inc(S["yb"], 1)
                        for e in range(NE):
                            for q in range(2):
                                nxt = e * 2 + q + 1
                                if nxt < NMM:
                                    hidden(nxt // 2, nxt % 2)
                                output(e, q)

                    pairs = GROUPS // 2
                    group(0, 0)
                    group(1, 0)
                    with pe.Fori(1, pairs) as n:
                        group(0, n)
                        group(1, n)
                    group(0, pairs)

                @block.scalar
                def _(act):
                    A = nc.scalar

                    def group(u, n):
                        g = 2 * n + u
                        act.wait_ge(S["link"], g * LINKS + 5)
                        A.activation(wl[:, :, :, :], wl[:, :, :, :], ACT.Exp).then_inc(S["wexp"], 1)
                        for i in range(GB):
                            act.wait_ge(S["t1"], g * GB + i + 1)
                            if i >= 2:
                                act.wait_ge(S["g"], g * GB + i - 1)
                            A.copy(oT[:, i % 2].rearrange("p k n -> p (k n)"), bank[i % 2][:, 0:KC * P]).then_inc(S["t1c"], 1)
                        act.wait_ge(S["link"], g * LINKS + 19)
                        A.activation(sd[:, :], mv[:, :, 1], ACT.Sqrt, bias=eps_sb[:, 0:1]).then_inc(S["sd"], 1)
                        for i in range(GB):
                            act.wait_ge(S["t2"], g * GB + i + 1)
                            A.copy(xnT[:, :, i * P:(i + 1) * P], bank[i % 2][:, 0:KC * P].rearrange("p (k n) -> p k n", k=KC)).then_inc(S["t2c"], 1)
                        act.wait_ge(S["link"], g * LINKS + 25)
                        A.activation(ex[:, :, :], dif[:, :, :], ACT.Exp).then_inc(S["y0"], 1)
                        for i in range(GB):
                            act.wait_ge(S["stp"], g * GB + i + 1)
                            A.copy(cT[:, i, :], bank[i % 2][0:NE, 0:P]).then_inc(S["ctc"], 1)
                        for e in range(NE):
                            for q in range(2):
                                m = e * 2 + q
                                for f in range(KC):
                                    act.wait_ge(S["h1"], (g * NMM + m) * KC + f + 1)
                                    if m >= 2:
                                        act.wait_ge(S["y2"], g * NE * GB + (m - 2) // 2 * GB + (4 if m % 2 == 0 else GB))
                                    A.activation(hT[:, q, f, 0:HALF[q][1] * P], bank[4 + f][:, 0:HALF[q][1] * P], ACT.Gelu,
                                                 bias=b1_sb[:, e, f:f + 1]).then_inc(S["act"], 1)

                    pairs = GROUPS // 2
                    group(0, 0)
                    group(1, 0)
                    with act.Fori(1, pairs) as n:
                        group(0, n)
                        group(1, n)
                    group(0, pairs)


_INS = ['x', 'src', 'dst', 'L0_gnn_W', 'L0_gnn_attn', 'L0_gnn_W_out', 'L0_ffn_router_w', 'L0_ffn_w1', 'L0_ffn_b1', 'L0_ffn_w2', 'L0_ffn_b2']
_OUTS = [((6250, 256), 'float32')]


def kernel(**inputs):
    import numpy as _np
    import concourse.bacc as _bacc
    from concourse import mybir as _mybir
    from concourse.bass_utils import run_bass_kernel_spmd as _run

    nc = _bacc.Bacc("TRN2", target_bir_lowering=False, num_devices=1)
    arrays, args = {}, []
    for name in _INS:
        a = _np.ascontiguousarray(inputs[name])
        arrays[f"in_{name}_dram"] = a
        args.append(nc.dram_tensor(f"in_{name}_dram", a.shape, _mybir.dt.from_np(a.dtype), kind="ExternalInput").ap())
    for i, (shape, dtype) in enumerate(_OUTS):
        dt = _mybir.dt.from_np(_np.dtype(dtype))
        args.append(nc.dram_tensor(f"out_{i}_dram", shape, dt, kind="ExternalOutput").ap())
    gnn_ffn_kernel(nc, *args)
    r = _run(nc, [arrays], core_ids=[0])
    got = tuple(r.results[0][f"out_{i}_dram"] for i in range(len(_OUTS)))
    return got[0]
```

```python
from contextlib import ExitStack

import concourse.bass as bass
from concourse import mybir

F32 = mybir.dt.float32
F32R = mybir.dt.float32r
I32 = mybir.dt.int32
U32 = mybir.dt.uint32
ALU = mybir.AluOpType
ACT = mybir.ActivationFunctionType
AX = mybir.AxisListType.X

P = 128
BIG = 1.0e30
EPS = 1e-5


class Cfg:

    def __init__(self, x, src, W, rw):
        self.N, self.D = x.shape
        self.E = src.shape[0]
        self.H, _, self.DH = W.shape
        self.NE = rw.shape[0]
        self.NB = -(-self.N // P)
        self.TAIL = self.N - (self.NB - 1) * P
        self.BT = 16
        self.NT = -(-self.E // (P * self.BT)) * self.BT
        self.NBAT = self.NT // self.BT
        self.KC = self.D // P
        self.HW = self.DH + 1
        self.ROW = self.H * self.HW
        self.G = -(-self.NT // P)


def gnn_ffn_kernel(nc, x, src, dst, W, attn, W_out, rw, w1, b1, w2, b2, out):
    c = Cfg(x, src, W, rw)
    N, D, E, H, DH, NE, NB, NT, BT, NBAT = c.N, c.D, c.E, c.H, c.DH, c.NE, c.NB, c.NT, c.BT, c.NBAT
    KC, HW, ROW, G, TAIL = c.KC, c.HW, c.ROW, c.G, c.TAIL
    RING = 3
    WIDE = ROW + H
    ZW = BT * H
    full_tiles = E // P
    rest = E - full_tiles * P
    gl = G - 1
    last_full = full_tiles - gl * P
    GB = 7
    GROUPS = NB // GB
    assert GROUPS * GB == NB and G <= P
    L2BASE = NT * P
    L3BASE = L2BASE + G * P
    NONE = L3BASE + P
    LOOK = 2 * P + 4

    def internal(name, shape):
        return nc.dram_tensor(name, shape, F32, kind="Internal").ap()

    table = internal("table", (NB * P, WIDE))
    flag1_d = internal("flag1_d", (NT, 2 * P))
    flag2_d = internal("flag2_d", (G, 2 * P))
    flag3_d = internal("flag3_d", (1, 2 * P))
    last_d = internal("last_d", (G * P,))
    look_d = internal("look_d", (G * P, LOOK))
    start_d = internal("start_d", (G * P * P, H))
    part_d = internal("part_d", (NONE + 1, WIDE))

    with ExitStack() as ctx:
        def sb(name, shape, dt=F32):
            return ctx.enter_context(nc.sbuf_tensor(name, shape, dt))

        def sem(name):
            return ctx.enter_context(nc.semaphore(name))

        bank = [ctx.enter_context(nc.psum_tensor(f"bank{i}", [P, 512], F32)) for i in range(8)]

        ident = sb("ident", [P, P])
        wout_sb = sb("wout_sb", [P, KC, D])
        w1h, w1l, w2h, w2l = (sb(n, [P, NE, KC, D], F32R) for n in ("w1h", "w1l", "w2h", "w2l"))
        b1_sb = sb("b1_sb", [P, NE, KC])
        b2_sb = sb("b2_sb", [NE, D])
        rwr = sb("rwr", [NE, D])
        rwh = sb("rwh", [P, KC, NE], F32R)
        rwl = sb("rwl", [P, KC, NE], F32R)
        eps_sb = sb("eps_sb", [P, 1])
        ones = sb("ones", [1, P])
        rowsN = sb("rowsN", [P, 3, NB + GB], I32)
        mid = ExitStack()
        ctx.enter_context(mid)

        def sb(name, shape, dt=F32):
            return mid.enter_context(nc.sbuf_tensor(name, shape, dt))

        srcC = sb("srcC", [P, G * P], I32)
        rankC = sb("rankC", [P, G * P])
        startC = sb("startC", [P, G * P])
        rank2C = sb("rank2C", [P, G])
        start2C = sb("start2C", [P, G])
        rank3C = sb("rank3C", [P, 1])
        start3C = sb("start3C", [P, 1])
        De = sb("De", [P, NT, H])

        pre = ExitStack()
        ctx.enter_context(pre)

        def s1(name, shape, dt=F32):
            return pre.enter_context(nc.sbuf_tensor(name, shape, dt))

        dN = s1("dN", [P, NB, H])
        offN = s1("offN", [P, NB])
        cF = s1("cF", [P, NB])
        nodecol = s1("nodecol", [P, NB])
        firstI = s1("firstI", [P, G], I32)
        start = s1("start", [P, G, P])
        nofirst = s1("nofirst", [P, G, P])
        with ExitStack() as st:
            def s1(name, shape, dt=F32):
                return st.enter_context(nc.sbuf_tensor(name, shape, dt))

            def sem1(name):
                return st.enter_context(nc.semaphore(name))

            xall = s1("xall", [P, NB, D])
            dstI = s1("dstI", [P, G, P], I32)
            srcI = s1("srcI", [P, G, P], I32)
            dstF = s1("dstF", [P, G, P])
            early_rows = s1("early_rows", [P, max(2 * G * P, GB * LOOK)])
            srcF, rank = (early_rows[:, i * G * P:(i + 1) * G * P].rearrange("p (g e) -> p g e", g=G) for i in range(2))
            prevI = s1("prevI", [P, G], I32)
            prevF = s1("prevF", [P, G])
            cont = s1("cont", [P, G])
            kF = s1("kF", [P, G, 2, P])
            key2 = s1("key2", [P, G])
            tcol = s1("tcol", [P, G])
            base2 = s1("base2", [P, G])
            k2r = s1("k2r", [G, 1, P])
            start2 = s1("start2", [G, 1, P])
            rank2 = s1("rank2", [G, 1, P])
            kF2 = s1("kF2", [G, 1, 2, P])
            k3r = s1("k3r", [1, 1, P])
            gi = s1("gi", [1, P])
            eq3 = s1("eq3", [1, G])
            last2 = s1("last2", [1, G])
            start3 = s1("start3", [1, 1, P])
            rank3 = s1("rank3", [1, 1, P])
            kF3 = s1("kF3", [1, 1, 2, P])
            rec3 = s1("rec3", [1, 2, G])
            rec = s1("rec", [P, G, 4])
            place = De[:, :, :].rearrange("p t h -> p (t h)")
            lastrow = place[:, 0:NT]
            junk = place[:, NT:3 * NT].rearrange("p (u t) -> p u t", u=2)
            junk2 = place[:, 3 * NT:3 * NT + 3 * P].rearrange("p (u e) -> p u e", u=3)
            zeros = place[:, 3 * NT + 3 * P:3 * NT + 5 * P]
            half_node = s1("half_node", [P, NB])
            none_row = s1("none_row", [1, WIDE])
            wcat = s1("wcat", [P, KC, WIDE])
            wraw = s1("wraw", [P, KC, H, DH])
            attb = s1("attb", [P, H, 2 * DH])
            wprod = s1("wprod", [P, KC, H, DH])
            stat = s1("stat", [P, NB, 6])
            mv = s1("mv", [P, NB, 2])
            sd = s1("sd", [P, NB])
            rstd = s1("rstd", [P, NB])
            xn1 = s1("xn1", [P, 2, D])
            xnT = s1("xnT", [P, 2, KC, P])
            hrow = s1("hrow", [P, 2, WIDE])
            look0 = s1("look0", [P, GB, LOOK])
            look2 = [look0[:, :, :], early_rows[:, 0:GB * LOOK].rearrange("p (i e) -> p i e", i=GB)]
            lookI = s1("lookI", [P, 2, GB], I32)
            cG = s1("cG", [P, 2, GB])
            nid = s1("nid", [P, GB])
            sums = s1("sums", [P, 3, GB])
            here = s1("here", [P, 3, GB])
            pos = s1("pos", [P, GB])
            offI = s1("offI", [P, GB], I32)
            dS = s1("dS", [P, GB, H])
            look_ix, lk, sums_ok, off_ok, put_ok, put, zero_ok, zero_st, hold, hold_d, off_i, lk0 = (
                sem1(n) for n in ("look_ix", "lk", "sums_ok", "off_ok", "put_ok", "put", "zero_ok", "zero_st", "hold", "hold_d", "off_i", "lk0"))
            looked = [sem1(f"looked{u}") for u in range(2)]
            NOWHERE = 2 * G * P * P
            (pads, ld_x, ld_e, ld_w, ld_ffn, ident_ok, iota_ok, dv, count_ok, idx_t, key2_ok, key2_t, rank2_ok, rank2_t,
             rw_t, rw_copied, prep_ok, prep_st, last_ld, var_ok, sd_ok, xn_ok, w_ok, tr_done,
             tr_copied, h_done, h_copied, d_copied) = (sem1(n) for n in (
                "pads", "ld_x", "ld_e", "ld_w", "ld_ffn", "ident_ok", "iota_ok", "dv", "count_ok", "idx_t", "key2_ok",
                "key2_t", "rank2_ok", "rank2_t", "rw_t", "rw_copied", "prep_ok", "prep_st",
                "last_ld", "var_ok", "sd_ok", "xn_ok", "w_ok", "tr_done", "tr_copied", "h_done", "h_copied", "d_copied"))
            row_st = [sem1(f"row_st{u}") for u in range(2)]

            e_rows = lambda a: a[0:gl * P * P].rearrange("(g q e) -> q g e", q=P, e=P)
            n_pads = 4
            n_edge_loads = 7 + gl
            n_ffn_loads = 3

            with nc.Block() as block:
                @block.sync
                def _(sp):
                    with nc.allow_non_contiguous_dma(reason="tile borders"):
                        sp.dma_start(dstI[:, 0:gl, :], e_rows(dst)).then_inc(ld_e, 16)
                        sp.dma_start(srcI[:, 0:gl, :], e_rows(src)).then_inc(ld_e, 16)
                        sp.wait_ge(pads, n_pads)
                        for t, a in ((dstI, dst), (srcI, src)):
                            sp.dma_start(t[0:last_full, gl, :],
                                         a[gl * P * P:full_tiles * P].rearrange("(q e) -> q e", e=P)).then_inc(ld_e, 16)
                            sp.dma_start(t[last_full:last_full + 1, gl, 0:rest],
                                         a[full_tiles * P:E].rearrange("(q e) -> q e", q=1)).then_inc(ld_e, 16)
                        col = lambda lo, n: dst[lo:lo + (n - 1) * P + 1:P].rearrange("(q o) -> q o", o=1)
                        sp.dma_start(prevI[1:P, 0:1], col(P - 1, P - 1)).then_inc(ld_e, 16)
                        for g in range(1, gl):
                            sp.dma_start(prevI[:, g:g + 1], col(g * P * P - 1, P)).then_inc(ld_e, 16)
                        sp.dma_start(prevI[0:last_full + 1, gl:G], col(gl * P * P - 1, last_full + 1)).then_inc(ld_e, 16)
                        sp.wait_ge(prep_ok, 1)
                        sp.dma_start(last_d.rearrange("(g q) -> q g", q=P), dstF[:, :, P - 1]).then_inc(last_ld, 16)
                        sp.wait_ge(last_ld, 16)
                        sp.dma_start(lastrow[:, :], last_d[0:NT].partition_broadcast(P)).then_inc(last_ld, 16)
                        sp.wait_ge(zero_ok, 1)
                        sp.dma_start(start_d.rearrange("(p c e) h -> p c (e h)", p=P, e=2 * P // H),
                                     zeros.unsqueeze(1).to_broadcast([P, G * P * H // (2 * P), 2 * P])).then_inc(zero_st, 16)
                        sp.wait_ge(prep_ok, 2)
                        sp.dma_start(flag1_d[0:gl * P, :].rearrange("(g q) e -> q g e", q=P),
                                     kF[:, 0:gl].rearrange("q g s e -> q g (s e)")).then_inc(prep_st, 16)
                        sp.dma_start(flag1_d[gl * P:NT, :], kF[0:NT - gl * P, gl].rearrange("q s e -> q (s e)")).then_inc(prep_st, 16)
                        look_v = look_d.rearrange("(g q) e -> q g e", q=P)
                        sp.dma_start(look_v[:, :, 0:P], dstF[:, :, :]).then_inc(prep_st, 16)
                        sp.dma_start(look_v[:, :, P:2 * P], start[:, :, :]).then_inc(prep_st, 16)
                        sp.wait_ge(prep_ok, 3)
                        sp.dma_start(flag2_d, kF2[:, 0].rearrange("g s e -> g (s e)")).then_inc(prep_st, 16)
                        sp.dma_start(flag3_d, kF3[:, 0].rearrange("g s e -> g (s e)")).then_inc(prep_st, 16)
                        sp.dma_start(look_d[0:P - 1, 2 * P:LOOK], rec[1:P, 0, :]).then_inc(prep_st, 16)
                        for g in range(1, G):
                            sp.dma_start(look_d[g * P - 1:(g + 1) * P - 1, 2 * P:LOOK], rec[:, g, :]).then_inc(prep_st, 16)
                        sp.dma_start(look_d[G * P - 1:G * P, 2 * P:LOOK], rec[0:1, 0, :]).then_inc(prep_st, 16)
                        sp.dma_start(part_d[NONE:NONE + 1, :], none_row[:, :]).then_inc(prep_st, 16)

                    def store(u, n):
                        sp.wait_ge(h_copied, 2 * n + u + 1)
                        sp.dma_start(table[bass.ds((2 * n + u) * P, P), :], hrow[:, u, :]).then_inc(row_st[u], 16)
                    with sp.Fori(0, NB // 2) as n:
                        store(0, n)
                        store(1, n)
                    store(0, NB // 2)
                    sp.wait_ge(row_st[0], 16 * (NB // 2 + 1))
                    sp.wait_ge(row_st[1], 16 * (NB // 2))
                    sp.wait_ge(prep_st, 16 * (8 + G))

                @block.gpsimd
                def _(pool):
                    nc.gpsimd.memset(ident[:], 0.0).then_inc(ident_ok, 1)
                    pool.wait_ge(ident_ok, 1)
                    nc.gpsimd.affine_select(out=ident[:], in_=ident[:], compare_op=ALU.not_equal, fill=1.0,
                                            base=0, pattern=[[-1, P]], channel_multiplier=1).then_inc(ident_ok, 1)
                    imp = dict(allow_small_or_imprecise_dtypes=True)
                    nc.gpsimd.iota(nodecol[:], pattern=[[P, NB]], base=0, channel_multiplier=1, **imp).then_inc(iota_ok, 1)
                    nc.gpsimd.iota(tcol[:], pattern=[[P, G]], base=1, channel_multiplier=1, **imp).then_inc(iota_ok, 1)
                    nc.gpsimd.iota(base2[:], pattern=[[P, G]], base=L2BASE, channel_multiplier=0, **imp).then_inc(iota_ok, 1)
                    nc.gpsimd.iota(gi[:], pattern=[[1, P]], base=1, channel_multiplier=0, **imp).then_inc(iota_ok, 1)
                    nc.gpsimd.memset(eps_sb[:], EPS).then_inc(iota_ok, 1)
                    nc.gpsimd.memset(ones[:], 1.0).then_inc(iota_ok, 1)
                    nc.gpsimd.memset(nofirst[:], 1.0).then_inc(iota_ok, 1)
                    nc.gpsimd.memset(none_row[:, 0:ROW], 0.0).then_inc(iota_ok, 1)
                    nc.gpsimd.memset(none_row[:, ROW:WIDE], -BIG).then_inc(iota_ok, 1)
                    pool.wait_ge(iota_ok, 9)
                    nc.gpsimd.memset(nofirst[:, :, 0], 0.0).then_inc(iota_ok, 1)
                    pool.wait_ge(ident_ok, 2)
                    nc.gpsimd.tensor_scalar(half_node[:], nodecol[:], -1.0, 0.5, ALU.mult, ALU.add).then_inc(iota_ok, 1)
                    nc.gpsimd.memset(zeros, 0.0).then_inc(zero_ok, 1)
                    pool.wait_ge(iota_ok, 11)

                    def find(u, n):
                        pool.wait_ge(look_ix, 2 * n + u + 1)
                        pool.sem_inc(hold, 1)
                        for i in range(GB):
                            pool.indirect_dma_start(out=look2[u][:, i, :], out_offset=None, in_=look_d[:, :],
                                                    in_offset=bass.IndirectOffsetOnAxis(ap=lookI[:, u, i:i + 1], axis=0)).then_inc(looked[u], 16)

                    def scatter(g):
                        pool.wait_ge(put_ok, g + 1)
                        pool.sem_inc(hold, 1)
                        for i in range(GB):
                            pool.indirect_dma_start(out=start_d[:, :], out_offset=bass.IndirectOffsetOnAxis(ap=offI[:, i:i + 1], axis=0),
                                                    in_=dS[:, i, :], in_offset=None, bounds_check=G * P * P - 1,
                                                    oob_is_err=False).then_inc(put, 16)

                    pool.wait_ge(prep_st, 16 * (8 + G))
                    find(0, 0)
                    find(1, 0)
                    pool.wait_ge(zero_st, 16)
                    find(0, 1)
                    scatter(0)
                    with pool.Fori(1, GROUPS // 2) as n:
                        find(1, n)
                        scatter(2 * n - 1)
                        find(0, n + 1)
                        scatter(2 * n)
                    scatter(GROUPS - 2)
                    scatter(GROUPS - 1)
                    pool.wait_ge(put, 16 * NB)

                @block.vector
                def _(dve):
                    n_dv = [0]

                    def link(ins):
                        n_dv[0] += 1
                        ins.then_inc(dv, 1)
                        dve.wait_ge(dv, n_dv[0])

                    v = nc.vector

                    def runs(key, first_, flags_, rank_, reset):
                        flat = lambda a: a.rearrange("p n e -> p (n e)")
                        link(v.memset(first_[:, :, 0], 1.0))
                        link(v.tensor_tensor(first_[:, :, 1:P], key[:, :, 1:P], key[:, :, 0:P - 1], ALU.not_equal))
                        link(v.tensor_scalar(flags_[:, :, 0, :], first_[:, :, :], -BIG, None, ALU.mult))
                        link(v.memset(flags_[:, :, 1, 0], -BIG))
                        link(v.tensor_scalar(flags_[:, :, 1, 1:P], first_[:, :, P - 1:0:-1], -BIG, None, ALU.mult))
                        link(v.tensor_tensor_scan(flat(rank_), flat(reset), flat(first_), 0.0, ALU.mult, ALU.add))
                        link(v.tensor_scalar(flat(rank_), flat(rank_), -1.0, None, ALU.add))

                    v.memset(dstI[:, gl, :], 8191).then_inc(pads, 1)
                    v.memset(srcI[:, gl, :], 0).then_inc(pads, 1)
                    v.memset(prevI[:, :], -5).then_inc(pads, 1)
                    v.memset(xall[:, NB - 1, :], 0.0).then_inc(pads, 1)
                    dve.wait_ge(ld_e, 16 * n_edge_loads)
                    link(v.tensor_copy(dstF[:, :, :], dstI[:, :, :]))
                    dve.sem_inc(prep_ok, 1)
                    link(v.tensor_copy(srcF[:, :, :], srcI[:, :, :]))
                    link(v.tensor_copy(prevF[:, :], prevI[:, :]))
                    dve.wait_ge(iota_ok, 10)
                    runs(dstF[:, :, :], start[:, :, :], kF[:, :, :, :], rank[:, :, :], nofirst[:, :, :])
                    dve.sem_inc(prep_ok, 1)
                    link(v.tensor_tensor(cont[:, :], dstF[:, :, 0], prevF[:, :], ALU.is_equal))
                    link(v.tensor_tensor(key2[:, :], dstF[:, :, 0], tcol[:, :], ALU.add))
                    link(v.tensor_tensor(key2[:, :], key2[:, :], cont[:, :], ALU.mult))
                    link(v.tensor_tensor(key2[:, :], key2[:, :], tcol[:, :], ALU.subtract))
                    dve.sem_inc(key2_ok, 1)
                    dve.wait_ge(ld_w, 16 * (2 + H))
                    for s in range(2):
                        link(v.tensor_tensor(wprod[:, :, :, :], wraw[:, :, :, :],
                                             attb[:, :, s * DH:(s + 1) * DH].unsqueeze(1).to_broadcast([P, KC, H, DH]), ALU.mult))
                        o = wcat[:, :, 0:ROW].rearrange("p c (h w) -> p c h w", h=H)[:, :, :, DH] if s == 0 else wcat[:, :, ROW:WIDE]
                        link(v.tensor_reduce(o, wprod[:, :, :, :], AX, ALU.add))
                    for k in range(KC):
                        link(v.tensor_copy(wcat[:, k, 0:ROW].rearrange("p (h w) -> p h w", h=H)[:, :, 0:DH], wraw[:, k]))
                    dve.sem_inc(w_ok, 1)
                    dve.wait_ge(idx_t, 3 * G)
                    for j, o in enumerate((rankC, startC, srcC)):
                        for g in range(G):
                            m = j * G + g
                            link(v.tensor_copy(o[:, g * P:(g + 1) * P], bank[m // 4][:, (m % 4) * P:(m % 4 + 1) * P]))
                    dve.wait_ge(key2_t, 2)
                    link(v.tensor_copy(k2r[:, 0, :], bank[6][0:G, 0:P]))
                    link(v.tensor_copy(last2[:, :], bank[6][0:1, P:P + G]))
                    runs(k2r[:, :, :], start2[:, :, :], kF2[:, :, :, :], rank2[:, :, :], nofirst[0:G, 0:1, :])
                    link(v.tensor_scalar(k3r[:, 0, :], gi[:, :], -1.0, None, ALU.mult))
                    link(v.tensor_tensor(eq3[:, 1:G], key2[0:1, 1:G], last2[:, 0:G - 1], ALU.is_equal))
                    link(v.tensor_tensor(last2[:, 1:G], key2[0:1, 1:G], gi[:, 1:G], ALU.add))
                    link(v.tensor_tensor(last2[:, 1:G], last2[:, 1:G], eq3[:, 1:G], ALU.mult))
                    link(v.tensor_tensor(k3r[:, 0, 1:G], last2[:, 1:G], gi[:, 1:G], ALU.subtract))
                    runs(k3r[:, :, :], start3[:, :, :], kF3[:, :, :, :], rank3[:, :, :], nofirst[0:1, 0:1, :])
                    link(v.tensor_copy(rec3[:, 0, :], k3r[:, 0, 1:G + 1]))
                    link(v.tensor_scalar(rec3[:, 1, :], rank3[:, 0, 1:G + 1], float(L3BASE), None, ALU.add))
                    dve.sem_inc(rank2_ok, 1)
                    dve.wait_ge(rank2_t, 1)
                    link(v.tensor_copy(rank2C[:, :], bank[7][:, 0:G]))
                    link(v.tensor_copy(start2C[:, :], bank[7][:, 8:8 + G]))
                    link(v.tensor_copy(rank3C[:, :], bank[7][:, 16:17]))
                    link(v.tensor_copy(start3C[:, :], bank[7][:, 17:18]))
                    link(v.tensor_copy(rec[:, :, 0], dstF[:, :, 0]))
                    link(v.tensor_tensor(rec[:, :, 1], rank2C[:, :], base2[:, :], ALU.add))
                    link(v.tensor_copy(rec[:, :, 2:4], bank[7][:, 24:24 + 2 * G].rearrange("p (s g) -> p g s", s=2)))
                    dve.sem_inc(prep_ok, 1)
                    link(v.tensor_scalar(firstI[:, :], dstF[:, :, 0], float(NB * P - 1), None, ALU.min))
                    dve.wait_ge(rw_t, KC)
                    rwT = bank[7][:, 64:64 + KC * NE].rearrange("p (k e) -> p k e", k=KC)
                    link(v.tensor_copy(rwh[:, :, :], rwT))
                    link(v.tensor_tensor(rwl[:, :, :], rwT, rwh[:, :, :], ALU.subtract))
                    dve.wait_ge(ld_x, 16 * 2)
                    with dve.Fori(0, NB // GB) as q:
                        for i in range(GB):
                            b = q * GB + i
                            v.bn_stats(stat[:, bass.ds(b, 1), :].rearrange("p a s -> p (a s)"),
                                       xall[:, bass.ds(b, 1), :].rearrange("p a d -> p (a d)")).then_inc(var_ok, 1)
                    dve.wait_ge(var_ok, NB)
                    link(v.tensor_tensor(mv[:, :, 0], stat[:, :, 1], stat[:, :, 4], ALU.add))
                    link(v.tensor_tensor(mv[:, :, 1], stat[:, :, 1], stat[:, :, 4], ALU.subtract))
                    link(v.tensor_scalar(mv[:, :, 0], mv[:, :, 0], 0.5, None, ALU.mult))
                    link(v.tensor_tensor(mv[:, :, 1], mv[:, :, 1], mv[:, :, 1], ALU.mult))
                    link(v.tensor_tensor(stat[:, :, 2], stat[:, :, 2], stat[:, :, 5], ALU.add))
                    link(v.tensor_scalar(mv[:, :, 1], mv[:, :, 1], 0.25, None, ALU.mult))
                    link(v.scalar_tensor_tensor(mv[:, :, 1], stat[:, :, 2], 1.0 / D, mv[:, :, 1], ALU.mult, ALU.add))
                    dve.sem_inc(var_ok, 1)
                    def ask(u, n):
                        g = 2 * n + u
                        dve.wait_ge(count_ok, (g + 1) * GB)
                        v.tensor_scalar(cG[:, u, :], cF[:, bass.ds(g * GB, GB)], -0.5, 0.5 * NT, ALU.mult, ALU.add).then_inc(off_ok, 1)
                        dve.wait_ge(off_ok, g + 1)
                        v.tensor_copy(lookI[:, u, :], cG[:, u, :]).then_inc(look_ix, 1)

                    ALINKS = 17

                    def answer(u, n, part):
                        g = 2 * n + u
                        look = look2[u]
                        b0 = g * GB
                        cnt = [0 if part == 0 else 1]

                        def link(ins):
                            cnt[0] += 1
                            ins.then_inc(lk, 1)
                            dve.wait_ge(lk, g * ALINKS + cnt[0])

                        if part == 0:
                            dve.sem_inc(hold_d, 1)
                            link(v.tensor_copy(nid[:, :], nodecol[:, bass.ds(b0, GB)]))
                            dve.wait_ge(looked[u], 16 * GB * (n + 1))
                        if part < GB:
                            i = part
                            d_, s_ = look[:, i, 0:P], look[:, i, P:2 * P]
                            if i > 0:
                                dve.wait_ge(sums_ok, g * 3 * GB + 3 * i)
                            v.tensor_scalar(junk2[:, 0, :], d_, nid[:, i:i + 1], 0.0, ALU.is_lt, ALU.add, accum_out=sums[:, 0, i:i + 1]).then_inc(sums_ok, 1)
                            v.scalar_tensor_tensor(junk2[:, 1, :], d_, nid[:, i:i + 1], s_, ALU.is_lt, ALU.mult, accum_out=sums[:, 1, i:i + 1]).then_inc(sums_ok, 1)
                            v.tensor_scalar(junk2[:, 2, :], d_, nid[:, i:i + 1], 0.0, ALU.is_equal, ALU.add, accum_out=sums[:, 2, i:i + 1]).then_inc(sums_ok, 1)
                            return
                        dve.wait_ge(sums_ok, (g + 1) * 3 * GB)
                        link(v.tensor_scalar(here[:, 0, :], sums[:, 2, :], 1.0, None, ALU.min))
                        link(v.tensor_tensor(here[:, 1, :], look[:, :, 2 * P], nid[:, :], ALU.is_equal))
                        link(v.tensor_tensor(here[:, 1, :], here[:, 1, :], here[:, 0, :], ALU.mult))
                        link(v.tensor_tensor(here[:, 2, :], look[:, :, 2 * P + 2], nid[:, :], ALU.is_equal))
                        link(v.tensor_tensor(here[:, 2, :], here[:, 2, :], here[:, 1, :], ALU.mult))
                        link(v.tensor_scalar(pos[:, :], cG[:, u, :], float(P), None, ALU.mult))
                        link(v.tensor_tensor(sums[:, 0, :], sums[:, 0, :], pos[:, :], ALU.add))
                        link(v.tensor_tensor(sums[:, 1, :], sums[:, 1, :], pos[:, :], ALU.add))
                        for k, a in enumerate((sums[:, 1, :], look[:, :, 2 * P + 1], look[:, :, 2 * P + 3])):
                            link(v.scalar_tensor_tensor(junk2[:, k, 0:GB], a, -float(NONE), here[:, k, :], ALU.add, ALU.mult))
                            link(v.tensor_scalar(rowsN[:, k, bass.ds(b0, GB)], junk2[:, k, 0:GB], float(NONE), None, ALU.add))
                        link(v.scalar_tensor_tensor(pos[:, :], sums[:, 0, :], -float(NOWHERE), here[:, 0, :], ALU.add, ALU.mult))
                        link(v.tensor_scalar(offN[:, bass.ds(b0, GB)], pos[:, :], float(NOWHERE), None, ALU.add))
                        assert cnt[0] == ALINKS, cnt

                    def post(g, fresh=False):
                        dve.wait_ge(d_copied, (g + 1) * GB)
                        if not fresh:
                            dve.wait_ge(put, 16 * GB * g)
                        dve.sem_inc(hold_d, 1)
                        v.tensor_copy(offI[:, :], offN[:, bass.ds(g * GB, GB)]).then_inc(off_i, 1)
                        dve.wait_ge(off_i, g + 1)
                        v.tensor_copy(dS[:, :, :], dN[:, bass.ds(g * GB, GB), :]).then_inc(put_ok, 1)

                    v.memset(rowsN[:, :, NB:NB + GB], 0).then_inc(lk0, 1)
                    ask(0, 0)
                    ask(1, 0)
                    for part in range(GB + 1):
                        answer(0, 0, part)
                    dve.wait_ge(sd_ok, 1)
                    link(v.reciprocal(rstd[:, :], sd[:, :]))

                    def norm(b, u, fresh=False):
                        if not fresh:
                            dve.wait_ge(tr_done, b - 1)
                        xb = xall[:, bass.ds(b, 1), :].rearrange("p a d -> p (a d)")
                        v.tensor_scalar(xn1[:, u, :], xb, mv[:, bass.ds(b, 1), 0], rstd[:, bass.ds(b, 1)],
                                        ALU.subtract, ALU.mult).then_inc(xn_ok, 1)

                    def rows(u, n):
                        dve.wait_ge(h_done, 2 * n + u + 1)
                        if not (isinstance(n, int) and n == 0):
                            dve.wait_ge(row_st[u], 16 * n)
                        v.tensor_copy(hrow[:, u, :], bank[6 + u][:, 0:WIDE]).then_inc(h_copied, 1)
                        v.tensor_copy(dN[:, bass.ds(2 * n + u, 1), :].rearrange("p a h -> p (a h)"),
                                      bank[6 + u][:, ROW:WIDE]).then_inc(d_copied, 1)

                    dve.sem_inc(rw_copied, 1)
                    norm(0, 0, True)
                    norm(1, 1, True)
                    norm(2, 0)
                    rows(0, 0)
                    norm(3, 1)
                    rows(1, 0)

                    def two(n, group, parts):
                        norm(2 * n + 2, 0)
                        rows(0, n)
                        answer(*group, parts[0])
                        norm(2 * n + 3, 1)
                        rows(1, n)
                        answer(*group, parts[1])

                    PAIRS = 4
                    assert GB + 1 == 2 * PAIRS and 1 + (GROUPS - 2) * PAIRS <= NB // 2 - 1

                    def round_(q, group, after, fresh=False):
                        ask(*after)
                        for j in range(PAIRS):
                            two(q * PAIRS + 1 + j, group, (2 * j, 2 * j + 1))
                        post(q, fresh)

                    round_(0, (1, 0), (0, 1), True)
                    with dve.Fori(1, GROUPS // 2) as k:
                        round_(2 * k - 1, (0, k), (1, k))
                        round_(2 * k, (1, k), (0, k + 1))
                    for n in range(1 + (GROUPS - 2) * PAIRS, NB // 2 - 1):
                        j = n - 1 - (GROUPS - 2) * PAIRS
                        two(n, (0, GROUPS // 2), (2 * j, 2 * j + 1))
                    norm(NB - 1, 0)
                    rows(0, NB // 2 - 1)
                    rows(1, NB // 2 - 1)
                    post(GROUPS - 2)
                    for part in range(2 * (NB // 2 - 2 - (GROUPS - 2) * PAIRS), GB + 1):
                        answer(0, GROUPS // 2, part)
                    rows(0, NB // 2)
                    post(GROUPS - 1)
                    dve.wait_ge(lk0, 1)

                @block.tensor
                def _(pe):
                    T = nc.tensor
                    pe.wait_ge(ident_ok, 2)
                    pe.wait_ge(prep_ok, 2)
                    for j, a in enumerate((rank, start, srcF)):
                        for g in range(G):
                            m = j * G + g
                            T.transpose(bank[m // 4][:, (m % 4) * P:(m % 4 + 1) * P], a[:, g, :], ident[:]).then_inc(idx_t, 1)
                    pe.wait_ge(key2_ok, 1)
                    T.transpose(bank[6][0:G, 0:P], key2[:, :], ident[:]).then_inc(key2_t, 1)
                    T.matmul(bank[6][0:1, P:P + G], ident[:, P - 1:P], key2[:, :], start=True, stop=True).then_inc(key2_t, 1)
                    pe.wait_ge(rank2_ok, 1)
                    T.transpose(bank[7][:, 0:G], rank2[:, 0, :], ident[0:G, 0:G])
                    T.transpose(bank[7][:, 8:8 + G], start2[:, 0, :], ident[0:G, 0:G])
                    T.transpose(bank[7][:, 16:17], rank3[:, 0, :], ident[0:1, 0:1])
                    T.transpose(bank[7][:, 17:18], start3[:, 0, :], ident[0:1, 0:1])
                    T.matmul(bank[7][:, 24:24 + 2 * G], ones[:, :], rec3[:, :, :].rearrange("p s g -> p (s g)"),
                             start=True, stop=True).then_inc(rank2_t, 1)
                    pe.wait_ge(prep_ok, 3)
                    pe.wait_ge(ld_ffn, 16 * n_ffn_loads)
                    for k in range(KC):
                        T.transpose(bank[7][:, 64 + k * NE:64 + (k + 1) * NE], rwr[:, k * P:(k + 1) * P], ident[0:NE, 0:NE]).then_inc(rw_t, 1)
                    pe.wait_ge(w_ok, 1)
                    pe.wait_ge(rw_copied, 1)
                    def turn(u, n):
                        pe.wait_ge(xn_ok, 2 * n + u + 1)
                        if not (isinstance(n, int) and n == 0):
                            pe.wait_ge(tr_copied, 2 * n + u - 1)
                        for k in range(KC):
                            t = nc.tensor.transpose(bank[4 + u][:, k * P:(k + 1) * P],
                                                    xn1[:, u, k * P:(k + 1) * P], ident[:])
                        t.then_inc(tr_done, 1)

                    def product(u, n):
                        pe.wait_ge(tr_copied, 2 * n + u + 1)
                        if not (isinstance(n, int) and n == 0):
                            pe.wait_ge(h_copied, 2 * n + u - 1)
                            pe.wait_ge(d_copied, 2 * n + u - 1)
                        for k in range(KC):
                            m = nc.tensor.matmul(bank[6 + u][:, 0:WIDE], xnT[:, u, k, :], wcat[:, k, :], start=k == 0, stop=k == KC - 1)
                        m.then_inc(h_done, 1)

                    turn(0, 0)
                    turn(1, 0)
                    product(0, 0)
                    turn(0, 1)
                    product(1, 0)
                    turn(1, 1)
                    with pe.Fori(1, NB // 2 - 1) as n:
                        product(0, n)
                        turn(0, n + 1)
                        product(1, n)
                        turn(1, n + 1)
                    m = NB // 2 - 1
                    product(0, m)
                    turn(0, m + 1)
                    product(1, m)
                    product(0, m + 1)

                @block.scalar
                def _(act):
                    nc_x = x[0:(NB - 1) * P, :].rearrange("(b p) d -> p b d", p=P)
                    for h in range(H):
                        act.dma_start(wraw[:, :, h, :], W[h].rearrange("(k p) d -> p k d", p=P)).then_inc(ld_w, 16)
                    act.dma_start(attb[:, :, :], attn.partition_broadcast(P)).then_inc(ld_w, 16)
                    act.dma_start(wout_sb[:, :, :], W_out.rearrange("(k p) n -> p k n", p=P)).then_inc(ld_w, 16)
                    act.dma_start(xall[:, 0:NB - 1, :], nc_x).then_inc(ld_x, 16)
                    act.wait_ge(pads, n_pads)
                    act.dma_start(xall[0:TAIL, NB - 1, :], x[(NB - 1) * P:N, :]).then_inc(ld_x, 16)
                    act.dma_start(rwr[:, :], rw).then_inc(ld_ffn, 16)
                    act.dma_start(b2_sb[:, :], b2).then_inc(ld_ffn, 16)
                    with nc.allow_non_contiguous_dma(reason="biases by partition"):
                        act.dma_start(b1_sb[:, :, :].rearrange("p e k -> p (e k)"), b1.rearrange("e (k p) -> p (e k)", p=P)).then_inc(ld_ffn, 16)
                    act.wait_ge(iota_ok, 11)
                    act.wait_ge(last_ld, 32)

                    def count(b, u):
                        nc.scalar.activation(junk[:, u, :], lastrow[:, :], ACT.Sign, bias=half_node[:, bass.ds(b, 1)],
                                             accum_out=cF[:, bass.ds(b, 1)]).then_inc(count_ok, 1)

                    count(0, 0)
                    count(1, 1)
                    with act.Fori(1, NB // 2) as n:
                        for u in range(2):
                            act.wait_ge(count_ok, 2 * n + u - 1)
                            count(2 * n + u, u)
                    act.wait_ge(count_ok, NB - 2)
                    count(NB - 1, 0)
                    act.wait_ge(var_ok, NB + 1)
                    act.wait_ge(iota_ok, 10)
                    nc.scalar.activation(sd[:, :], mv[:, :, 1], ACT.Sqrt, bias=eps_sb[:, 0:1]).then_inc(sd_ok, 1)

                    def copies(u, n):
                        act.wait_ge(tr_done, 2 * n + u + 1)
                        if not (isinstance(n, int) and n == 0):
                            act.wait_ge(h_done, 2 * n + u - 1)
                        nc.scalar.copy(xnT[:, u].rearrange("p k n -> p (k n)"), bank[4 + u][:, 0:KC * P]).then_inc(tr_copied, 1)

                    copies(0, 0)
                    copies(1, 0)
                    copies(0, 1)
                    copies(1, 1)
                    with act.Fori(1, NB // 2 - 1) as n:
                        copies(0, n + 1)
                        copies(1, n + 1)
                    m = NB // 2 - 1
                    copies(0, m + 1)

        with ExitStack() as st:
            def s2(name, shape, dt=F32):
                return st.enter_context(nc.sbuf_tensor(name, shape, dt))

            def sem2(name):
                return st.enter_context(nc.semaphore(name))

            fr = s2("fr", [P, G, WIDE])
            keep = s2("keep", [P, G, P])
            fill_done = sem2("fill_done")
            spread = s2("spread", [P, G, P, H])
            filled = s2("filled", [P, G, P, H])
            first_ld, spread_ld, first_ok, fill_ok, fill_t = (
                sem2(n) for n in ("first_ld", "spread_ld", "first_ok", "fill_ok", "fill_t"))

            with nc.Block() as block:
                @block.sync
                def _(sp):
                    sp.dma_start(spread[:, :, :, :].rearrange("p g e h -> p g (e h)"),
                                 start_d.rearrange("(g q e) h -> q g (e h)", q=P, e=P)).then_inc(spread_ld, 16)
                    sp.wait_ge(spread_ld, 16)

                @block.gpsimd
                def _(pool):
                    for g in range(G):
                        pool.indirect_dma_start(out=fr[:, g, :], out_offset=None, in_=table[:, :],
                                                in_offset=bass.IndirectOffsetOnAxis(ap=firstI[:, g:g + 1], axis=0)).then_inc(first_ld, 16)

                @block.vector
                def _(dve):
                    v = nc.vector
                    dve.wait_ge(spread_ld, 16)
                    dve.wait_ge(first_ld, 16 * G)
                    v.tensor_copy(spread[:, :, 0, :], fr[:, :, ROW:WIDE]).then_inc(first_ok, 1)
                    link_ = v.tensor_scalar(keep[:, :, :], start[:, :, :], -1.0, 1.0, ALU.mult, ALU.add)
                    link_.then_inc(first_ok, 1)
                    dve.wait_ge(first_ok, 2)
                    flat = lambda a: a.rearrange("p g e -> p (g e)")
                    for h in range(H):
                        v.tensor_tensor_scan(flat(filled[:, :, :, h]), flat(keep[:, :, :]), flat(spread[:, :, :, h]), 0.0,
                                             ALU.mult, ALU.add).then_inc(fill_ok, 1)
                    for h in range(H):
                        for g in range(G):
                            m = h * G + g
                            if m % 4 == 0:
                                dve.wait_ge(fill_t, m // 4 + 1)
                            n_ = min(P, NT - g * P)
                            v.tensor_copy(De[:, g * P:g * P + n_, h], bank[m // 4 % 8][:, (m % 4) * P:(m % 4) * P + n_]).then_inc(fill_done, 1)
                    dve.wait_ge(fill_done, H * G)

                @block.tensor
                def _(pe):
                    for h in range(H):
                        pe.wait_ge(fill_ok, h + 1)
                        for g in range(G):
                            m = h * G + g
                            t = nc.tensor.transpose(bank[m // 4 % 8][:, (m % 4) * P:(m % 4 + 1) * P], filled[:, g, :, h], ident[:])
                            if m % 4 == 3:
                                t.then_inc(fill_t, 1)
        pre.close()

        with ExitStack() as st:
            def s3(name, shape, dt=F32):
                return st.enter_context(nc.sbuf_tensor(name, shape, dt))

            def sem3(name):
                return st.enter_context(nc.semaphore(name))

            ring = s3("ring", [P, RING * BT, WIDE])
            ring4 = ring[:, :, 0:ROW].rearrange("p k (h w) -> p k h w", h=H)
            idx = s3("idx", [P, RING, BT], I32)
            flags = s3("flags", [ZW, RING, 2, P])
            ranks = s3("ranks", [P, P])
            z = s3("z", [P, ZW])
            eC = s3("eC", [P, ZW])
            f1 = s3("f1", [ZW, P])
            r1 = s3("r1", [ZW, P])
            rho = s3("rho", [ZW, P])
            arg = s3("arg", [P, ZW])
            w23 = s3("w23", [P, ZW])
            oh = s3("oh", [P, RING, BT, P])
            stage = s3("stage", [P, 2, 4, WIDE])
            wexp = s3("wexp", [P, NE, KC, D])
            w_ld, wh_ok, wl_ok = (sem3(n) for n in ("w_ld", "wh_ok", "wl_ok"))
            S = {n: sem3("b_" + n) for n in "z e oh eT f1 r1 rho rc ms arg al msg agg ev setup hold_pool hold_pe hold_act hold_sp".split()}
            idx_ld = [sem3(f"idx_ld{r}") for r in range(RING)]
            flag_ld = [sem3(f"flag_ld{r}") for r in range(RING)]
            gathered = [sem3(f"gathered{r}") for r in range(RING)]
            stored = [sem3(f"stored{r}") for r in range(2)]
            upper_ld = sem3("upper_ld")
            upper_zero = sem3("upper_zero")

            ROUNDS = NBAT // RING
            assert NBAT == ROUNDS * RING + 1 and BT == 16
            QUADS = BT // 4
            UPPER = [(G, flag2_d, rank2C, start2C, L2BASE), (1, flag3_d, rank3C, start3C, L3BASE)]
            quads = lambda tiles: -(-tiles // 4)
            before = [(NT, NBAT * QUADS), (NT + G, NBAT * QUADS + quads(G))]

            with nc.Block() as block:
                @block.sync
                def _(sp):
                    def fetch(r, n):
                        t0 = (RING * n + r) * BT
                        if not (isinstance(n, int) and n == 0):
                            sp.wait_ge(gathered[r], 16 * BT * n)
                            sp.sem_inc(S["hold_sp"], 1)
                            sp.wait_ge(S["rho"], RING * n + r - 2)
                            sp.sem_inc(S["hold_sp"], 1)
                        sp.dma_start(idx[:, r, :], srcC[:, bass.ds(t0, BT)]).then_inc(idx_ld[r], 16)
                        for s in range(2):
                            sp.dma_start(flags[:, r, s, :],
                                         flag1_d[bass.ds(t0, BT), s * P:(s + 1) * P].unsqueeze(1).to_broadcast([BT, H, P])).then_inc(flag_ld[r], 16)

                    def store(r, n):
                        beta = RING * n + r
                        for q in range(QUADS):
                            sp.wait_ge(S["ev"], beta * BT + 4 * q + 4)
                            sp.sem_inc(S["hold_sp"], 1)
                            sp.dma_start(part_d[bass.ds((beta * BT + 4 * q) * P, 4 * P), :].rearrange("(k s) w -> s k w", k=4),
                                         stage[:, q % 2]).then_inc(stored[q % 2], 16)

                    fetch(0, 0)
                    fetch(1, 0)
                    fetch(2, 0)
                    store(0, 0)
                    fetch(0, 1)
                    store(1, 0)
                    fetch(1, 1)
                    store(2, 0)
                    with sp.Fori(1, ROUNDS - 1) as n:
                        fetch(2, n)
                        store(0, n)
                        fetch(0, n + 1)
                        store(1, n)
                        fetch(1, n + 1)
                        store(2, n)
                    m = ROUNDS - 1
                    fetch(2, m)
                    store(0, m)
                    fetch(0, m + 1)
                    store(1, m)
                    store(2, m)
                    store(0, m + 1)
                    n_st = [NBAT * QUADS // 2] * 2
                    sp.wait_ge(S["rho"], NBAT)
                    for lv, (tiles, flag_d, _, _, base) in enumerate(UPPER):
                        for s in range(2):
                            sp.dma_start(flags[0:tiles * H, 1 + lv, s, :],
                                         flag_d[:, s * P:(s + 1) * P].unsqueeze(1).to_broadcast([tiles, H, P])).then_inc(upper_ld, 16)
                    sp.wait_ge(upper_zero, 1)
                    for u in range(2):
                        sp.wait_ge(stored[u], 16 * n_st[u])
                    tiles_below = part_d[0:NT * P, :].rearrange("(t s) w -> t s w", s=P)
                    sp.dma_start(ring[:, BT:BT + gl, :], tiles_below[0:gl * P, 0, :].rearrange("(g q) w -> q g w", q=P)).then_inc(upper_ld, 16)
                    sp.dma_start(ring[0:NT - gl * P, BT + gl, :], tiles_below[gl * P:NT, 0, :]).then_inc(upper_ld, 16)

                    def store_upper(lv):
                        tiles, _, _, _, base = UPPER[lv]
                        done = before[lv][0]
                        for q in range(quads(tiles)):
                            k = min(4, tiles - 4 * q)
                            sp.wait_ge(S["ev"], done + 4 * q + k)
                            u = q % 2
                            sp.dma_start(part_d[base + 4 * q * P:base + (4 * q + k) * P, :].rearrange("(k s) w -> s k w", k=k),
                                         stage[:, u, 0:k]).then_inc(stored[u], 16)
                            n_st[u] += 1
                        for u in range(2):
                            sp.wait_ge(stored[u], 16 * n_st[u])

                    store_upper(0)
                    sp.dma_start(ring[0:G, 2 * BT, :], part_d[L2BASE:L2BASE + G * P, :].rearrange("(t s) w -> t s w", s=P)[:, 0, :]).then_inc(upper_ld, 16)
                    store_upper(1)

                @block.gpsimd
                def _(pool):
                    nc.gpsimd.iota(ranks[:], pattern=[[1, P]], base=0, channel_multiplier=0,
                                   allow_small_or_imprecise_dtypes=True).then_inc(S["setup"], 1)

                    def gather(r, n):
                        pool.wait_ge(idx_ld[r], 16 * (n + 1))
                        if not (isinstance(n, int) and n == 0):
                            pool.wait_ge(S["agg"], BT * (RING * n + r - 2))
                        pool.sem_inc(S["hold_pool"], 1)
                        for k in range(BT):
                            pool.indirect_dma_start(out=ring[:, r * BT + k, :], out_offset=None, in_=table[:, :],
                                                    in_offset=bass.IndirectOffsetOnAxis(ap=idx[:, r, k:k + 1], axis=0)).then_inc(gathered[r], 16)
                    for r in range(RING):
                        gather(r, 0)
                    with pool.Fori(1, ROUNDS) as n:
                        for r in range(RING):
                            gather(r, n)
                    gather(0, ROUNDS)

                @block.vector
                def _(dve):
                    v = nc.vector
                    dve.wait_ge(S["setup"], 1)

                    def segment_max(count, rows_, eT, kf, kr):
                        dve.wait_ge(S["eT"], count)
                        v.tensor_tensor_scan(f1[0:rows_, :], kf, eT, -BIG, ALU.add, ALU.max).then_inc(S["f1"], 1)
                        v.tensor_tensor_scan(r1[0:rows_, ::-1], kr, eT[:, ::-1], -BIG, ALU.add, ALU.max).then_inc(S["r1"], 1)
                        dve.wait_ge(S["f1"], count)
                        dve.wait_ge(S["r1"], count)
                        v.tensor_tensor(rho[0:rows_, :], f1[0:rows_, :], r1[0:rows_, :], ALU.max).then_inc(S["rho"], 1)

                    def batch(r, n):
                        beta = RING * n + r
                        t0 = beta * BT
                        k0, k1 = r * BT, (r + 1) * BT
                        dve.wait_ge(gathered[r], 16 * BT * (n + 1))
                        v.tensor_tensor(z[:, :].rearrange("p (k h) -> p k h", h=H), ring4[:, k0:k1, :, DH],
                                        De[:, bass.ds(t0, BT), :], ALU.add).then_inc(S["z"], 1)
                        dve.wait_ge(S["z"], beta + 1)
                        v.scalar_tensor_tensor(eC[:, :], z[:, :], 0.2, z[:, :], ALU.mult, ALU.max).then_inc(S["e"], 1)
                        if not (isinstance(n, int) and n == 0):
                            dve.wait_ge(S["agg"], BT * (beta - 2))
                        v.tensor_tensor(oh[:, r, :, :], ranks[:, :].unsqueeze(1).to_broadcast([P, BT, P]),
                                        rankC[:, bass.ds(t0, BT)].unsqueeze(2).to_broadcast([P, BT, P]), ALU.is_equal).then_inc(S["oh"], 1)
                        dve.wait_ge(flag_ld[r], 32 * (n + 1))
                        segment_max(beta + 1, ZW, bank[4][0:ZW, 0:P], flags[:, r, 0, :], flags[:, r, 1, :])
                        dve.wait_ge(S["rc"], beta + 1)
                        rhoT = bank[5][:, 0:ZW].rearrange("p (k h) -> p k h", h=H)
                        v.tensor_tensor(arg[:, :], eC[:, :], bank[5][:, 0:ZW], ALU.subtract).then_inc(S["arg"], 1)
                        v.tensor_tensor(ring[:, k0:k1, ROW:WIDE], rhoT,
                                        startC[:, bass.ds(t0, BT)].unsqueeze(2).to_broadcast([P, BT, H]), ALU.mult).then_inc(S["ms"], 1)
                        dve.wait_ge(S["al"], beta + 1)
                        for q in range(QUADS):
                            m = ring4[:, k0 + 4 * q:k0 + 4 * q + 4, :, 0:DH]
                            v.tensor_tensor(m, m, ring4[:, k0 + 4 * q:k0 + 4 * q + 4, :, DH:HW].to_broadcast([P, 4, H, DH]),
                                            ALU.mult).then_inc(S["msg"], 1)

                    for r in range(RING):
                        batch(r, 0)
                    dve.wait_ge(wh_ok, 1)
                    v.tensor_tensor(w1l[:, :, :, :], wexp[:, :, :, :], w1h[:, :, :, :], ALU.subtract).then_inc(wl_ok, 1)
                    with dve.Fori(1, ROUNDS) as n:
                        for r in range(RING):
                            batch(r, n)
                    dve.wait_ge(wh_ok, 2)
                    v.tensor_tensor(w2l[:, :, :, :], wexp[:, :, :, :], w2h[:, :, :, :], ALU.subtract).then_inc(wl_ok, 1)
                    batch(0, ROUNDS)

                    dve.wait_ge(S["agg"], NT)
                    dve.wait_ge(wl_ok, 2)
                    v.memset(ring[:, BT:3 * BT, :], 0.0).then_inc(upper_zero, 1)
                    for lv, (tiles, _, rank_, start_, _) in enumerate(UPPER):
                        c_ = NBAT + lv + 1
                        k0 = (1 + lv) * BT
                        w = tiles * H
                        dve.wait_ge(upper_ld, 16 * (6 + lv))
                        v.tensor_copy(eC[:, 0:w].rearrange("p (k h) -> p k h", h=H), ring[:, k0:k0 + tiles, ROW:WIDE]).then_inc(S["e"], 1)
                        v.tensor_tensor(oh[:, 1 + lv, 0:tiles, :], ranks[:, :].unsqueeze(1).to_broadcast([P, tiles, P]),
                                        rank_[:, :].unsqueeze(2).to_broadcast([P, tiles, P]), ALU.is_equal).then_inc(S["oh"], 1)
                        segment_max(c_, w, bank[4][0:w, 0:P], flags[0:w, 1 + lv, 0, :], flags[0:w, 1 + lv, 1, :])
                        dve.wait_ge(S["rc"], c_)
                        v.tensor_tensor(arg[:, 0:w], eC[:, 0:w], bank[5][:, 0:w], ALU.subtract).then_inc(S["arg"], 1)
                        v.tensor_tensor(ring[:, k0:k0 + tiles, ROW:WIDE], bank[5][:, 0:w].rearrange("p (k h) -> p k h", h=H),
                                        start_[:, :].unsqueeze(2).to_broadcast([P, tiles, H]), ALU.mult).then_inc(S["ms"], 1)
                        dve.wait_ge(S["al"], c_)
                        for q in range(quads(tiles)):
                            k = min(4, tiles - 4 * q)
                            m = ring4[:, k0 + 4 * q:k0 + 4 * q + k, :, :]
                            v.tensor_tensor(m, m, w23[:, 16 * q:16 * q + 4 * k].rearrange("p (k h) -> p k h", h=H).unsqueeze(3).to_broadcast([P, k, H, HW]),
                                            ALU.mult).then_inc(S["msg"], 1)

                @block.tensor
                def _(pe):
                    T = nc.tensor

                    def turns(count, w, hold):
                        pe.wait_ge(S["e"], count)
                        if hold:
                            pe.sem_inc(S["hold_pe"], 1)
                        T.transpose(bank[4][0:w, 0:P], eC[:, 0:w], ident[:]).then_inc(S["eT"], 1)
                        pe.wait_ge(S["rho"], count)
                        if hold:
                            pe.sem_inc(S["hold_pe"], 1)
                        T.transpose(bank[5][:, 0:w], rho[0:w, :], ident[0:w, 0:w]).then_inc(S["rc"], 1)

                    def sums(r, tiles, n_agg, n_msg, fresh):
                        for k in range(tiles):
                            if k % 4 == 0:
                                pe.wait_ge(S["msg"], n_msg + k // 4 + 1)
                            if not (fresh and k < 4):
                                pe.wait_ge(S["ev"], n_agg + k - 3)
                            T.matmul(bank[k % 4][:, 0:WIDE], oh[:, r, k, :], ring[:, r * BT + k, :], start=True, stop=True).then_inc(S["agg"], 1)

                    def batch(r, n):
                        beta = RING * n + r
                        turns(beta + 1, ZW, True)
                        sums(r, BT, beta * BT, beta * QUADS, isinstance(n, int) and n == 0 and r == 0)

                    for r in range(RING):
                        batch(r, 0)
                    with pe.Fori(1, ROUNDS) as n:
                        for r in range(RING):
                            batch(r, n)
                    batch(0, ROUNDS)
                    for lv, (tiles, _, _, _, _) in enumerate(UPPER):
                        turns(NBAT + lv + 1, tiles * H, False)
                        sums(1 + lv, tiles, before[lv][0], before[lv][1], False)

                @block.scalar
                def _(act):
                    A = nc.scalar

                    def evacuate(k, done, quad_uses):
                        act.wait_ge(S["agg"], done + k + 1)
                        if k % 4 == 0 and quad_uses is not None:
                            act.wait_ge(stored[k // 4 % 2], 16 * quad_uses)
                        A.copy(stage[:, k // 4 % 2, k % 4, :], bank[k % 4][:, 0:WIDE]).then_inc(S["ev"], 1)

                    def batch(r, n):
                        beta = RING * n + r
                        act.wait_ge(S["arg"], beta + 1)
                        A.activation(ring4[:, r * BT:(r + 1) * BT, :, DH], arg[:, :].rearrange("p (k h) -> p k h", h=H), ACT.Exp).then_inc(S["al"], 1)
                        first = isinstance(n, int) and n == 0 and r == 0
                        for k in range(BT):
                            evacuate(k, beta * BT, None if first and k < 8 else 2 * beta + k // 8)

                    act.dma_start(wexp[:, :, :, :], w1.rearrange("e (k p) n -> p e k n", p=P)).then_inc(w_ld, 16)
                    for r in range(RING):
                        batch(r, 0)
                    act.wait_ge(w_ld, 16)
                    A.copy(w1h[:, :, :, :], wexp[:, :, :, :]).then_inc(wh_ok, 1)
                    act.wait_ge(wl_ok, 1)
                    act.dma_start(wexp[:, :, :, :], w2.rearrange("e (k p) n -> p e k n", p=P)).then_inc(w_ld, 16)
                    with act.Fori(1, ROUNDS) as n:
                        for r in range(RING):
                            batch(r, n)
                    act.wait_ge(w_ld, 32)
                    A.copy(w2h[:, :, :, :], wexp[:, :, :, :]).then_inc(wh_ok, 1)
                    batch(0, ROUNDS)
                    uses = [NBAT * QUADS // 2] * 2
                    for lv, (tiles, _, _, _, _) in enumerate(UPPER):
                        act.wait_ge(S["arg"], NBAT + lv + 1)
                        A.activation(w23[:, 0:tiles * H], arg[:, 0:tiles * H], ACT.Exp).then_inc(S["al"], 1)
                        for k in range(tiles):
                            evacuate(k, before[lv][0], uses[k // 4 % 2])
                        for q in range(quads(tiles)):
                            uses[q % 2] += 1

        mid.close()

        with ExitStack() as st:
            def s4(name, shape, dt=F32):
                return st.enter_context(nc.sbuf_tensor(name, shape, dt))

            xg = s4("xg", [P, 2, GB, D])
            x1 = s4("x1", [P, GB, D])
            xn = s4("xn", [P, GB, D])
            y = s4("y", [P, 2, GB, D])
            on = s4("on", [P, GB, D])
            oT = s4("oT", [P, 2, KC, P])
            xTh = s4("xTh", [P, 2, KC, GB * P], F32R)
            xTl = s4("xTl", [P, 2, KC, GB * P], F32R)
            hT = s4("hT", [P, 2, KC, 512])
            hTh = s4("hTh", [P, 2, KC, 512], F32R)
            hTl = s4("hTl", [P, 2, KC, 512], F32R)
            pa = s4("pa", [P, 3, GB, WIDE])
            rowI = s4("rowI", [P, 3, GB], I32)
            mx = s4("mx", [P, GB, H])
            wl = s4("wl", [P, 3, GB, H])
            den = s4("den", [P, GB, H])
            rden = s4("rden", [P, GB, H])
            stat = s4("stat4", [P, GB, 6])
            mv = s4("mv4", [P, GB, 2])
            sd = s4("sd4", [P, GB])
            rstd = s4("rstd4", [P, GB])
            lg = s4("lg", [P, GB, NE])
            top = s4("top", [P, GB, 8])
            topi = s4("topi", [P, GB, 8], U32)
            topf = s4("topf", [P, GB, 2])
            ex = s4("ex", [P, GB, NE + 2])
            dif = s4("dif", [P, GB, NE + 2])
            sm = s4("sm", [P, GB])
            rsm = s4("rsm", [P, GB])
            pr = s4("pr", [P, GB, 2])
            ps = s4("ps", [P, GB])
            rps = s4("rps", [P, GB])
            wt = s4("wt", [P, GB, 2])
            cmb = s4("cmb", [P, 2, GB, NE])
            cmb2 = s4("cmb2", [P, GB, NE])
            cT = s4("cT", [NE, GB * P])
            iota8 = s4("iota8", [P, NE])
            S = {n: st.enter_context(nc.semaphore("f_" + n)) for n in
                 "t1 t1c o g x1 stats sd xn t2 t2h t2l lg tops cmb ct ctc exps yi yb yba h1 gelu hh hl y2 yacc wlink link iota last scaled rescaled hold ask wexp hold_pool".split()}
            fetched = st.enter_context(nc.semaphore("fetched"))
            x_ld = [st.enter_context(nc.semaphore(f"x_ld{r}")) for r in range(2)]
            y_st = [st.enter_context(nc.semaphore(f"y_st{r}")) for r in range(2)]
            HALF = [(0, 4), (4, GB - 4)]
            STEPS = NE * len(HALF)
            OUTS = NE * GB
            pairs = GROUPS // 2
            assert GROUPS == 2 * pairs + 1 and pairs >= 2
            WLINKS = 5
            K_DEN, K_VAR, K_RSTD, K_DIF, LINKS = 2, 9, 10, 14, 25
            TURN, COPY, PROJECT, ASK, RESIDUAL = 5, 6, 7, 7, 8
            NORM, TURN2 = 15, 18
            WEIGH = 26
            ROUTE = 27
            outs_before = lambda m: m // 2 * GB + (HALF[0][1] if m % 2 else 0)

            def begins(u, n):
                return isinstance(n, int) and n == 0 and u == 0

            def early(n):
                return isinstance(n, int) and n == 0

            with nc.Block() as block:
                @block.sync
                def _(sp):
                    def load(u, n, rows_last=P):
                        g = 2 * n + u
                        if not early(n):
                            sp.wait_ge(S["x1"], (g - 1) * GB)
                        r0_ = g * GB * P
                        k = GB - 1
                        sp.dma_start(xg[:, u, 0:k, :], x[bass.ds(r0_, k * P), :].rearrange("(b p) d -> p b d", p=P)).then_inc(x_ld[u], 16)
                        sp.dma_start(xg[0:rows_last, u, k, :], x[bass.ds(r0_ + k * P, rows_last), :]).then_inc(x_ld[u], 16)

                    def store(u, n, rows_last=P):
                        g = 2 * n + u
                        sp.wait_ge(S["last"], g + 1)
                        r0_ = g * GB * P
                        k = GB - 1
                        sp.dma_start(out[bass.ds(r0_, k * P), :].rearrange("(b p) d -> p b d", p=P), y[:, u, 0:k, :]).then_inc(y_st[u], 16)
                        sp.dma_start(out[bass.ds(r0_ + k * P, rows_last), :], y[0:rows_last, u, k, :]).then_inc(y_st[u], 16)

                    load(0, 0)
                    load(1, 0)
                    with sp.Fori(1, pairs) as n:
                        load(0, n)
                        store(0, n - 1)
                        load(1, n)
                        store(1, n - 1)
                    load(0, pairs, TAIL)
                    store(0, pairs - 1)
                    store(1, pairs - 1)
                    store(0, pairs, TAIL)
                    sp.wait_ge(y_st[0], 32 * (pairs + 1))
                    sp.wait_ge(y_st[1], 32 * pairs)

                @block.gpsimd
                def _(pool):
                    def fetch(g):
                        pool.wait_ge(S["ask"], g + 1)
                        pool.sem_inc(S["hold_pool"], 1)
                        for k in range(3):
                            for i in range(GB):
                                pool.indirect_dma_start(out=pa[:, k, i, :], out_offset=None, in_=part_d[:, :],
                                                        in_offset=bass.IndirectOffsetOnAxis(ap=rowI[:, k, i:i + 1], axis=0)).then_inc(fetched, 16)
                    nc.gpsimd.iota(iota8[:], pattern=[[1, NE]], base=0, channel_multiplier=0,
                                   allow_small_or_imprecise_dtypes=True).then_inc(S["iota"], 1)

                    def merge(g):
                        gp = nc.gpsimd
                        lv = [pa[:, k, :, 0:ROW].rearrange("p b (h w) -> p b h w", h=H) for k in range(3)]
                        pool.wait_ge(S["wexp"], g + 1)
                        gp.tensor_tensor(lv[0], lv[0], wl[:, 0].unsqueeze(3).to_broadcast([P, GB, H, HW]), ALU.mult).then_inc(S["scaled"], 1)
                        for k in range(1, 3):
                            pool.wait_ge(S["scaled"], g * 3 + k)
                            pool.wait_ge(S["rescaled"], g * 2 + k)
                            gp.tensor_tensor(pa[:, 0, :, 0:ROW], pa[:, 0, :, 0:ROW], pa[:, k, :, 0:ROW], ALU.add).then_inc(S["scaled"], 1)
                        pool.wait_ge(S["link"], g * LINKS + K_DEN)
                        gp.tensor_tensor(on[:, :, :].rearrange("p b (h w) -> p b h w", h=H), lv[0][:, :, :, 0:DH],
                                         rden[:, :, :].unsqueeze(3).to_broadcast([P, GB, H, DH]), ALU.mult).then_inc(S["o"], 1)

                    with pool.Fori(0, GROUPS) as g:
                        fetch(g)
                        merge(g)
                    fetch(GROUPS)

                @block.vector
                def _(dve):
                    v = nc.vector
                    dve.wait_ge(S["iota"], 1)

                    def ask(g):
                        v.tensor_copy(rowI[:, :, :], rowsN[:, :, bass.ds(g * GB, GB)]).then_inc(S["ask"], 1)

                    ask(0)

                    def weigh(g):
                        lm = [pa[:, k, :, ROW:WIDE] for k in range(3)]
                        dve.wait_ge(fetched, 16 * 3 * GB * (g + 1))
                        for j, args in enumerate([(mx[:, :, :], lm[0], lm[1], ALU.max), (mx[:, :, :], mx[:, :, :], lm[2], ALU.max)]
                                                 + [(wl[:, k], lm[k], mx[:, :, :], ALU.subtract) for k in range(3)]):
                            v.tensor_tensor(*args).then_inc(S["wlink"], 1)
                            dve.wait_ge(S["wlink"], g * WLINKS + j + 1)

                    def prepare(u, n, p):
                        g = 2 * n + u
                        cnt = [{NORM: K_DEN, NORM + 2: K_VAR,
                                ROUTE + 1: K_RSTD, ROUTE + 3: K_DIF}.get(p, 0)]

                        def link(ins):
                            cnt[0] += 1
                            ins.then_inc(S["link"], 1)
                            dve.wait_ge(S["link"], g * LINKS + cnt[0])

                        lv = pa[:, 0, :, 0:ROW].rearrange("p b (h w) -> p b h w", h=H)

                        if p in (0, 2):
                            k = 1 + p // 2
                            dve.wait_ge(S["wexp"], g + 1)
                            lv_ = pa[:, k, :, 0:ROW].rearrange("p b (h w) -> p b h w", h=H)
                            v.tensor_tensor(lv_, lv_, wl[:, k].unsqueeze(3).to_broadcast([P, GB, H, HW]), ALU.mult).then_inc(S["rescaled"], 1)
                        elif p == 4:
                            dve.wait_ge(S["scaled"], (g + 1) * 3)
                            link(v.tensor_scalar(den[:, :, :], lv[:, :, :, DH], 1e-8, None, ALU.add))
                            if not begins(u, n):
                                dve.wait_ge(S["t1"], g * GB)
                            link(v.reciprocal(rden[:, :, :], den[:, :, :]))
                            assert cnt[0] == K_DEN
                        elif p == ASK:
                            dve.wait_ge(S["o"], g + 1)
                            ask(g + 1)
                        if p == WEIGH:
                            weigh(g + 1)
                        if RESIDUAL <= p < RESIDUAL + GB:
                            i = p - RESIDUAL
                            if i == 0:
                                dve.wait_ge(x_ld[u], 32 * (n + 1))
                            dve.wait_ge(S["g"], g * GB + i + 1)
                            v.tensor_tensor(x1[:, i, :], xg[:, u, i, :], bank[2 + i % 2][:, 0:D], ALU.add).then_inc(S["x1"], 1)
                            dve.wait_ge(S["x1"], g * GB + i + 1)
                            v.bn_stats(stat[:, i, :], x1[:, i, :]).then_inc(S["stats"], 1)
                        elif p == NORM:
                            dve.wait_ge(S["stats"], (g + 1) * GB)
                            link(v.tensor_tensor(mv[:, :, 0], stat[:, :, 1], stat[:, :, 4], ALU.add))
                            link(v.tensor_tensor(mv[:, :, 1], stat[:, :, 1], stat[:, :, 4], ALU.subtract))
                            link(v.tensor_scalar(mv[:, :, 0], mv[:, :, 0], 0.5, None, ALU.mult))
                            link(v.tensor_tensor(mv[:, :, 1], mv[:, :, 1], mv[:, :, 1], ALU.mult))
                            link(v.tensor_tensor(stat[:, :, 2], stat[:, :, 2], stat[:, :, 5], ALU.add))
                            link(v.tensor_scalar(mv[:, :, 1], mv[:, :, 1], 0.25, None, ALU.mult))
                            link(v.scalar_tensor_tensor(mv[:, :, 1], stat[:, :, 2], 1.0 / D, mv[:, :, 1], ALU.mult, ALU.add))
                            assert cnt[0] == K_VAR
                        elif p == NORM + 2:
                            dve.wait_ge(S["sd"], g + 1)
                            link(v.reciprocal(rstd[:, :], sd[:, :]))
                            for i in range(GB):
                                v.tensor_scalar(xn[:, i, :], x1[:, i, :], mv[:, i, 0:1], rstd[:, i:i + 1], ALU.subtract, ALU.mult).then_inc(S["xn"], 1)
                        elif TURN2 + 1 <= p < TURN2 + 1 + GB:
                            i = p - TURN2 - 1
                            if i == 0 and not early(n):
                                dve.wait_ge(S["h1"], (g - 1) * STEPS * KC)
                            dve.wait_ge(S["t2h"], g * GB + i + 1)
                            v.tensor_tensor(xTl[:, u, :, i * P:(i + 1) * P], bank[i % 2][:, 0:KC * P].rearrange("p (k n) -> p k n", k=KC),
                                            xTh[:, u, :, i * P:(i + 1) * P], ALU.subtract).then_inc(S["t2l"], 1)
                        elif p == ROUTE + 1:
                            dve.wait_ge(S["lg"], g + 1)
                            link(v.tensor_copy(lg[:, :, :], bank[2][:, 0:GB * NE].rearrange("p (b e) -> p b e", b=GB)))
                            dve.sem_inc(S["hold"], 1)
                            for i in range(GB):
                                v.max(top[:, i, :], lg[:, i, :]).then_inc(S["tops"], 1)
                            dve.wait_ge(S["tops"], g * 2 * GB + GB)
                            dve.sem_inc(S["hold"], 1)
                            for i in range(GB):
                                v.max_index(topi[:, i, :], top[:, i, :], lg[:, i, :]).then_inc(S["tops"], 1)
                            dve.wait_ge(S["tops"], (g + 1) * 2 * GB)
                            link(v.tensor_copy(topf[:, :, :], topi[:, :, 0:2]))
                            link(v.tensor_tensor(dif[:, :, 0:NE], lg[:, :, :], top[:, :, 0:1].to_broadcast([P, GB, NE]), ALU.subtract))
                            link(v.tensor_tensor(dif[:, :, NE:NE + 2], top[:, :, 0:2], top[:, :, 0:1].to_broadcast([P, GB, 2]), ALU.subtract))
                            assert cnt[0] == K_DIF
                        elif p == ROUTE + 3:
                            dve.wait_ge(S["exps"], g + 1)
                            link(v.tensor_reduce(sm[:, :], ex[:, :, 0:NE], AX, ALU.add))
                            link(v.reciprocal(rsm[:, :], sm[:, :]))
                            link(v.tensor_tensor(pr[:, :, :], ex[:, :, NE:NE + 2], rsm[:, :].unsqueeze(2).to_broadcast([P, GB, 2]), ALU.mult))
                            link(v.tensor_reduce(ps[:, :], pr[:, :, :], AX, ALU.add))
                            link(v.tensor_scalar(ps[:, :], ps[:, :], 1e-12, None, ALU.max))
                            link(v.reciprocal(rps[:, :], ps[:, :]))
                            link(v.tensor_tensor(wt[:, :, :], pr[:, :, :], rps[:, :].unsqueeze(2).to_broadcast([P, GB, 2]), ALU.mult))
                            for k, o in ((0, cmb[:, u]), (1, cmb2[:, :, :])):
                                link(v.tensor_tensor(o, iota8[:, :].unsqueeze(1).to_broadcast([P, GB, NE]),
                                                     topf[:, :, k:k + 1].to_broadcast([P, GB, NE]), ALU.is_equal))
                                link(v.tensor_tensor(o, o, wt[:, :, k:k + 1].to_broadcast([P, GB, NE]), ALU.mult))
                            assert cnt[0] == LINKS
                            v.tensor_tensor(cmb[:, u], cmb[:, u], cmb2[:, :, :], ALU.add).then_inc(S["cmb"], 1)
                            dve.wait_ge(S["cmb"], g + 1)
                            if not early(n):
                                dve.wait_ge(y_st[u], 32 * n)
                            v.tensor_tensor(y[:, u], x1[:, :, :], xn[:, :, :], ALU.add).then_inc(S["yi"], 1)
                            dve.wait_ge(S["yi"], g + 1)

                    def rest(u, n, m):
                        g = 2 * n + u
                        if not (begins(u, n) and m < 2):
                            dve.wait_ge(S["y2"], g * OUTS + outs_before(m - 1))
                        for f in range(KC):
                            w = HALF[m % 2][1] * P
                            dve.wait_ge(S["hh"], (g * STEPS + m) * KC + f + 1)
                            v.tensor_tensor(hTl[:, m % 2, f, 0:w], hT[:, m % 2, f, 0:w], hTh[:, m % 2, f, 0:w], ALU.subtract).then_inc(S["hl"], 1)

                    def experts(u, n, after):
                        g = 2 * n + u
                        first = begins(u, n)
                        acc, bias = [0], [0]

                        def settled(later=0):
                            if not (first and acc[0] <= later):
                                dve.wait_ge(S["yacc"], g * OUTS + acc[0] - later)
                            if not (first and bias[0] == 0):
                                dve.wait_ge(S["yba"], g * GB + bias[0])

                        def accumulate(m):
                            h0, hn = HALF[m % 2]
                            e = m // 2
                            for i in range(h0, h0 + hn):
                                j = i - h0
                                dve.wait_ge(S["y2"], g * OUTS + outs_before(m) + min(j // 2 * 2 + 2, hn))
                                settled(GB - 1)
                                v.scalar_tensor_tensor(y[:, u, i, :], bank[6 + j // 2][:, j % 2 * D:(j % 2 + 1) * D], cmb[:, u, i, e:e + 1], y[:, u, i, :],
                                                       ALU.mult, ALU.add).then_inc(S["yacc"], 1)
                                acc[0] += 1

                        def point(p):
                            if p in (2, 4):
                                dve.wait_ge(S["yb"], g * GB + (4 if p == 2 else GB))
                            for i in {2: range(0, 4), 4: range(4, GB)}.get(p, ()):
                                settled()
                                v.tensor_tensor(y[:, u, i, :], y[:, u, i, :], bank[2 + i % 4 // 2][:, i % 2 * D:(i % 2 + 1) * D], ALU.add).then_inc(S["yba"], 1)
                                bias[0] += 1
                            if after:
                                prepare(*after, p)

                        for m in range(STEPS):
                            if m > 0:
                                rest(u, n, m)
                                accumulate(m - 1)
                            point(2 * m)
                            point(2 * m + 1)
                        if after:
                            rest(*after, 0)
                        accumulate(STEPS - 1)
                        dve.wait_ge(S["yacc"], (g + 1) * OUTS)
                        dve.sem_inc(S["last"], 1)

                    weigh(0)
                    for p in range(2 * STEPS):
                        prepare(0, 0, p)
                    rest(0, 0, 0)
                    experts(0, 0, (1, 0))
                    experts(1, 0, (0, 1))
                    with dve.Fori(1, pairs) as n:
                        experts(0, n, (1, n))
                        experts(1, n, (0, n + 1))
                    experts(0, pairs, None)

                @block.tensor
                def _(pe):
                    T = nc.tensor

                    def turn(i, src_, sem_):
                        for k in range(KC):
                            t = T.transpose(bank[i % 2][:, k * P:(k + 1) * P], src_[:, i, k * P:(k + 1) * P], ident[:])
                        t.then_inc(S[sem_], 1)

                    def exact(out_, lhs, rhs):
                        terms = [(lo, hi2) for (_, lo), (hi2, _) in zip(lhs, rhs)]
                        terms += [(hi, lo2) for (hi, _), (_, lo2) in zip(lhs, rhs)]
                        terms += [(hi, hi2) for (hi, _), (hi2, _) in zip(lhs, rhs)]
                        for j, (a, b) in enumerate(terms):
                            t = T.matmul(out_, a, b, start=j == 0, stop=j == len(terms) - 1)
                        return t

                    def prepare(u, n, p):
                        g = 2 * n + u
                        begin = begins(u, n)
                        if TURN <= p < TURN + GB:
                            i = p - TURN
                            if i == 0:
                                pe.wait_ge(S["o"], g + 1)
                                if not begin:
                                    pe.wait_ge(S["ctc"], g)
                            if i >= 2:
                                pe.wait_ge(S["t1c"], g * GB + i - 1)
                            turn(i, on, "t1")
                        if PROJECT <= p < PROJECT + GB:
                            i = p - PROJECT
                            pe.wait_ge(S["t1c"], g * GB + i + 1)
                            if i >= 2:
                                pe.wait_ge(S["x1"], g * GB + i - 1)
                            elif not begin:
                                pe.wait_ge(S["yba"], g * GB)
                            for k in range(KC):
                                t = T.matmul(bank[2 + i % 2][:, 0:D], oT[:, i % 2, k, :], wout_sb[:, k, :], start=k == 0, stop=k == KC - 1)
                            t.then_inc(S["g"], 1)
                        if TURN2 <= p < TURN2 + GB:
                            i = p - TURN2
                            pe.wait_ge(S["xn"], g * GB + i + 1)
                            if i < 2:
                                pe.wait_ge(S["t1c"], (g + 1) * GB)
                            else:
                                pe.wait_ge(S["t2l"], g * GB + i - 1)
                            turn(i, xn, "t2")
                        if p == ROUTE:
                            pe.wait_ge(S["t2l"], (g + 1) * GB)
                            pe.wait_ge(S["x1"], (g + 1) * GB)
                            for i in range(GB):
                                cols = slice(i * P, (i + 1) * P)
                                t = exact(bank[2][:, i * NE:(i + 1) * NE],
                                          [(xTh[:, u, k, cols], xTl[:, u, k, cols]) for k in range(KC)],
                                          [(rwh[:, k, :], rwl[:, k, :]) for k in range(KC)])
                            t.then_inc(S["lg"], 1)
                        if p == ROUTE + 4:
                            pe.wait_ge(S["cmb"], g + 1)
                            for i in range(GB):
                                t = T.transpose(bank[i // 4][0:NE, i % 4 * P:(i % 4 + 1) * P], cmb[:, u, i, :], ident[:])
                            t.then_inc(S["ct"], 1)

                    def hidden(u, n, m):
                        g = 2 * n + u
                        h0, hn = HALF[m % 2]
                        e = m // 2
                        if m == 0:
                            pe.wait_ge(S["t2l"], (g + 1) * GB)
                        for f in range(KC):
                            if not (begins(u, n) and m == 0):
                                pe.wait_ge(S["gelu"], (g * STEPS + m - 1) * KC + f + 1)
                            cols = slice(h0 * P, (h0 + hn) * P)
                            fs = slice(f * P, (f + 1) * P)
                            exact(bank[4 + f][:, 0:hn * P], [(w1h[:, e, k, fs], w1l[:, e, k, fs]) for k in range(KC)],
                                  [(xTh[:, u, k, cols], xTl[:, u, k, cols]) for k in range(KC)]).then_inc(S["h1"], 1)

                    def experts(u, n, after):
                        g = 2 * n + u
                        first = begins(u, n)

                        def output(m):
                            h0, hn = HALF[m % 2]
                            e = m // 2
                            pe.wait_ge(S["hl"], (g * STEPS + m + 1) * KC)
                            for i in range(hn):
                                if i % 2 == 0 and not (first and m == 0):
                                    pe.wait_ge(S["yacc"], g * OUTS + (outs_before(m - 1) + 2 if i == 0 else outs_before(m)))
                                cols = slice(i * P, (i + 1) * P)
                                exact(bank[6 + i // 2][:, i % 2 * D:(i % 2 + 1) * D], [(hTh[:, m % 2, f, cols], hTl[:, m % 2, f, cols]) for f in range(KC)],
                                      [(w2h[:, e, f, :], w2l[:, e, f, :]) for f in range(KC)]).then_inc(S["y2"], 1)

                        def point(p):
                            for i in {1: range(0, 4), 3: range(4, GB)}.get(p, ()):
                                if i == 0:
                                    pe.wait_ge(S["ctc"], g + 1)
                                if i == 4:
                                    pe.wait_ge(S["yba"], g * GB + 4)
                                T.matmul(bank[2 + i % 4 // 2][:, i % 2 * D:(i % 2 + 1) * D], cT[:, i * P:(i + 1) * P], b2_sb[:, :], start=True, stop=True).then_inc(S["yb"], 1)
                            if after:
                                prepare(*after, p)

                        for m in range(STEPS):
                            if m < STEPS - 1:
                                hidden(u, n, m + 1)
                            elif after:
                                hidden(*after, 0)
                            point(2 * m)
                            output(m)
                            point(2 * m + 1)

                    for p in range(2 * STEPS):
                        prepare(0, 0, p)
                    hidden(0, 0, 0)
                    experts(0, 0, (1, 0))
                    experts(1, 0, (0, 1))
                    with pe.Fori(1, pairs) as n:
                        experts(0, n, (1, n))
                        experts(1, n, (0, n + 1))
                    experts(0, pairs, None)

                @block.scalar
                def _(act):
                    A = nc.scalar

                    def weigh(g):
                        act.wait_ge(S["wlink"], (g + 1) * WLINKS)
                        A.activation(wl[:, :, :, :], wl[:, :, :, :], ACT.Exp).then_inc(S["wexp"], 1)

                    def prepare(u, n, p):
                        g = 2 * n + u
                        if COPY <= p < COPY + GB:
                            i = p - COPY
                            act.wait_ge(S["t1"], g * GB + i + 1)
                            if not (begins(u, n) and i < 2):
                                act.wait_ge(S["g"], g * GB + i - 1)
                            A.copy(oT[:, i % 2].rearrange("p k n -> p (k n)"), bank[i % 2][:, 0:KC * P]).then_inc(S["t1c"], 1)
                        if p == NORM + 1:
                            act.wait_ge(S["link"], g * LINKS + K_VAR)
                            A.activation(sd[:, :], mv[:, :, 1], ACT.Sqrt, bias=eps_sb[:, 0:1]).then_inc(S["sd"], 1)
                        if TURN2 + 1 <= p < TURN2 + 1 + GB:
                            i = p - TURN2 - 1
                            if i == 0 and not early(n):
                                act.wait_ge(S["h1"], (g - 1) * STEPS * KC)
                            act.wait_ge(S["t2"], g * GB + i + 1)
                            A.copy(xTh[:, u, :, i * P:(i + 1) * P], bank[i % 2][:, 0:KC * P].rearrange("p (k n) -> p k n", k=KC)).then_inc(S["t2h"], 1)
                        if p == ROUTE + 2:
                            weigh(g + 1)
                            act.wait_ge(S["link"], g * LINKS + K_DIF)
                            A.activation(ex[:, :, :], dif[:, :, :], ACT.Exp).then_inc(S["exps"], 1)

                    def experts(u, n, after):
                        g = 2 * n + u
                        first = begins(u, n)

                        def point(p):
                            if p == 0:
                                act.wait_ge(S["ct"], g + 1)
                                if not first:
                                    act.wait_ge(S["yb"], g * GB)
                                A.copy(cT[:, 0:4 * P], bank[0][0:NE, 0:4 * P])
                                A.copy(cT[:, 4 * P:GB * P], bank[1][0:NE, 0:(GB - 4) * P]).then_inc(S["ctc"], 1)
                            if after:
                                prepare(*after, p)

                        for m in range(STEPS):
                            w = HALF[m % 2][1] * P
                            for f in range(KC):
                                act.wait_ge(S["h1"], (g * STEPS + m) * KC + f + 1)
                                if not (first and m < 2):
                                    act.wait_ge(S["hl"], (g * STEPS + m - 2) * KC + f + 1)
                                A.activation(hT[:, m % 2, f, 0:w], bank[4 + f][:, 0:w], ACT.Gelu,
                                             bias=b1_sb[:, m // 2, f:f + 1]).then_inc(S["gelu"], 1)
                                if f == 0 and not (first and m < 2):
                                    act.wait_ge(S["y2"], g * OUTS + outs_before(m - 1))
                                act.wait_ge(S["gelu"], (g * STEPS + m) * KC + f + 1)
                                A.copy(hTh[:, m % 2, f, 0:w], hT[:, m % 2, f, 0:w]).then_inc(S["hh"], 1)
                            point(2 * m)
                            point(2 * m + 1)

                    weigh(0)
                    for p in range(2 * STEPS):
                        prepare(0, 0, p)
                    experts(0, 0, (1, 0))
                    experts(1, 0, (0, 1))
                    with act.Fori(1, pairs) as n:
                        experts(0, n, (1, n))
                        experts(1, n, (0, n + 1))
                    experts(0, pairs, None)


_INS = ['x', 'src', 'dst', 'L0_gnn_W', 'L0_gnn_attn', 'L0_gnn_W_out', 'L0_ffn_router_w', 'L0_ffn_w1', 'L0_ffn_b1', 'L0_ffn_w2', 'L0_ffn_b2']
_OUTS = [((6250, 256), 'float32')]


def kernel(**inputs):
    import numpy as _np
    import concourse.bacc as _bacc
    from concourse import mybir as _mybir
    from concourse.bass_utils import run_bass_kernel_spmd as _run

    nc = _bacc.Bacc("TRN2", target_bir_lowering=False, num_devices=1)
    arrays, args = {}, []
    for name in _INS:
        a = _np.ascontiguousarray(inputs[name])
        arrays[f"in_{name}_dram"] = a
        args.append(nc.dram_tensor(f"in_{name}_dram", a.shape, _mybir.dt.from_np(a.dtype), kind="ExternalInput").ap())
    for i, (shape, dtype) in enumerate(_OUTS):
        dt = _mybir.dt.from_np(_np.dtype(dtype))
        args.append(nc.dram_tensor(f"out_{i}_dram", shape, dt, kind="ExternalOutput").ap())
    gnn_ffn_kernel(nc, *args)
    r = _run(nc, [arrays], core_ids=[0])
    got = tuple(r.results[0][f"out_{i}_dram"] for i in range(len(_OUTS)))
    return got[0]
```
